# Optimizing a Trainium2 kernel written in Bass

```python
import numpy as np
import jax
import jax.numpy as jnp

def _softmax(x, axis=-1):
    return jax.nn.softmax(x, axis=axis)

def _gelu(x):
    return jax.nn.gelu(x, approximate=True)

def _silu(x):
    return jax.nn.silu(x)

def _sigmoid(x):
    return jax.nn.sigmoid(x)

def _layernorm(x, axis=-1, eps=1e-05):
    m = jnp.mean(x, axis=axis, keepdims=True)
    v = jnp.var(x, axis=axis, keepdims=True)
    return (x - m) / jnp.sqrt(v + eps)

def _scatter_add(tgt, idx, src, axis=0):
    return tgt.at[idx].add(src)

def _segment_sum(src, seg, n):
    return jax.ops.segment_sum(src, seg, n)
kernel_name = 'mk_sandwich_d1_jaxref_r4_70ec3f'

def setup_inputs(seed: int=0):
    np.random.seed(seed)
    _w = jnp.asarray

    def _L0_attn_setup():
        import jax, jax.numpy as jnp
        import numpy as np
        from jax import lax
        SPLIT = 8
        DIM = 16
        EPS = 1e-05

        def _branch(q, k, v, cw, cb, H_sp, W_sp, Hg, Wg):
            B, N, C = q.shape
            hd = C
            scale = hd ** (-0.5)
            wsz = H_sp * W_sp
            nh, nw = (Hg // H_sp, Wg // W_sp)

            def part(t):
                t = t.reshape(B, nh, H_sp, nw, W_sp, C).transpose(0, 1, 3, 2, 4, 5)
                return t.reshape(-1, wsz, 1, hd).transpose(0, 2, 1, 3)
            vimg = v.reshape(B, nh, H_sp, nw, W_sp, C).transpose(0, 1, 3, 5, 2, 4)
            vimg = vimg.reshape(-1, C, H_sp, W_sp)
            lepe = lax.conv_general_dilated(vimg, cw, (1, 1), [(1, 1), (1, 1)], dimension_numbers=('NCHW', 'OIHW', 'NCHW'), feature_group_count=C)
            lepe = lepe + cb[None, :, None, None]
            lepe = lepe.reshape(-1, 1, hd, wsz).transpose(0, 1, 3, 2)
            vw = vimg.reshape(-1, 1, hd, wsz).transpose(0, 1, 3, 2)
            attn = jax.nn.softmax(part(q) * scale @ jnp.swapaxes(part(k), -1, -2), axis=-1)
            out = attn @ vw + lepe
            out = out.transpose(0, 2, 1, 3).reshape(B, nh, nw, H_sp, W_sp, C)
            out = out.transpose(0, 1, 3, 2, 4, 5).reshape(B, N, C)
            return out
        key = jax.random.key(seed)
        ks = jax.random.split(key, 8)
        B, H, W = (8, 512, 512)
        d = DIM
        h = d // 2
        return {'x': jax.random.normal(ks[0], (B, H, W), jnp.float32), 'qkv_w': jax.random.normal(ks[1], (d, 3 * d), jnp.float32) * d ** (-0.5), 'conv_w0': jax.random.normal(ks[2], (h, 1, 3, 3), jnp.float32) * 0.3, 'conv_b0': jax.random.normal(ks[3], (h,), jnp.float32) * 0.02, 'conv_w1': jax.random.normal(ks[4], (h, 1, 3, 3), jnp.float32) * 0.3, 'conv_b1': jax.random.normal(ks[5], (h,), jnp.float32) * 0.02, 'proj_w': jax.random.normal(ks[6], (d, d), jnp.float32) * d ** (-0.5), 'proj_b': jax.random.normal(ks[7], (d,), jnp.float32) * 0.02, 'ln_w': jnp.ones((d,), jnp.float32), 'ln_b': jnp.zeros((d,), jnp.float32)}
    _L0_attn_in = _L0_attn_setup()

    def _L0_ffn_setup():
        import jax, jax.numpy as jnp
        import numpy as np
        HIDDEN = 512
        INTER = 2048
        B, S = (4, 256)

        def _qmatmul(x, w_int8, scale):
            y = jnp.einsum('bsh,ho->bso', x, w_int8.astype(x.dtype))
            return y * scale
        key = jax.random.key(seed)
        ks = jax.random.split(key, 7)
        x = jax.random.normal(ks[0], (B, S, HIDDEN), dtype=jnp.float32)
        w_gate = jax.random.randint(ks[1], (HIDDEN, INTER), -128, 128, dtype=jnp.int32).astype(jnp.int8)
        w_up = jax.random.randint(ks[2], (HIDDEN, INTER), -128, 128, dtype=jnp.int32).astype(jnp.int8)
        w_down = jax.random.randint(ks[3], (INTER, HIDDEN), -128, 128, dtype=jnp.int32).astype(jnp.int8)
        s_gate = jax.random.uniform(ks[4], (INTER,), dtype=jnp.float32) * 0.02 + 0.001
        s_up = jax.random.uniform(ks[5], (INTER,), dtype=jnp.float32) * 0.02 + 0.001
        s_down = jax.random.uniform(ks[6], (HIDDEN,), dtype=jnp.float32) * 0.02 + 0.001
        return {'x': x, 'w_gate': w_gate, 'w_up': w_up, 'w_down': w_down, 's_gate': s_gate, 's_up': s_up, 's_down': s_down}
    _L0_ffn_in = _L0_ffn_setup()
    _d = {'L0_attn_x': _L0_attn_in['x'], 'L0_attn_qkv_w': _L0_attn_in['qkv_w'], 'L0_attn_conv_w0': _L0_attn_in['conv_w0'], 'L0_attn_conv_b0': _L0_attn_in['conv_b0'], 'L0_attn_conv_w1': _L0_attn_in['conv_w1'], 'L0_attn_conv_b1': _L0_attn_in['conv_b1'], 'L0_attn_proj_w': _L0_attn_in['proj_w'], 'L0_attn_proj_b': _L0_attn_in['proj_b'], 'L0_attn_ln_w': _L0_attn_in['ln_w'], 'L0_attn_ln_b': _L0_attn_in['ln_b'], 'L0_ffn_w_gate': _L0_ffn_in['w_gate'], 'L0_ffn_w_up': _L0_ffn_in['w_up'], 'L0_ffn_w_down': _L0_ffn_in['w_down'], 'L0_ffn_s_gate': _L0_ffn_in['s_gate'], 'L0_ffn_s_up': _L0_ffn_in['s_up'], 'L0_ffn_s_down': _L0_ffn_in['s_down']}
    _x0 = _d['L0_attn_x']
    _d['L0_attn_x'] = jax.random.normal(jax.random.fold_in(jax.random.key(seed), 1), (4, 1024, 512), dtype=_x0.dtype)
    del _x0
    return _d

def reference(L0_attn_x, L0_attn_qkv_w, L0_attn_conv_w0, L0_attn_conv_b0, L0_attn_conv_w1, L0_attn_conv_b1, L0_attn_proj_w, L0_attn_proj_b, L0_attn_ln_w, L0_attn_ln_b, L0_ffn_w_gate, L0_ffn_w_up, L0_ffn_w_down, L0_ffn_s_gate, L0_ffn_s_up, L0_ffn_s_down):

    def _L0_attn_ref(x, qkv_w, conv_w0, conv_b0, conv_w1, conv_b1, proj_w, proj_b, ln_w, ln_b):
        import jax, jax.numpy as jnp
        import numpy as np
        from jax import lax
        SPLIT = 8
        DIM = 16
        EPS = 1e-05

        def _branch(q, k, v, cw, cb, H_sp, W_sp, Hg, Wg):
            B, N, C = q.shape
            hd = C
            scale = hd ** (-0.5)
            wsz = H_sp * W_sp
            nh, nw = (Hg // H_sp, Wg // W_sp)

            def part(t):
                t = t.reshape(B, nh, H_sp, nw, W_sp, C).transpose(0, 1, 3, 2, 4, 5)
                return t.reshape(-1, wsz, 1, hd).transpose(0, 2, 1, 3)
            vimg = v.reshape(B, nh, H_sp, nw, W_sp, C).transpose(0, 1, 3, 5, 2, 4)
            vimg = vimg.reshape(-1, C, H_sp, W_sp)
            lepe = lax.conv_general_dilated(vimg, cw, (1, 1), [(1, 1), (1, 1)], dimension_numbers=('NCHW', 'OIHW', 'NCHW'), feature_group_count=C)
            lepe = lepe + cb[None, :, None, None]
            lepe = lepe.reshape(-1, 1, hd, wsz).transpose(0, 1, 3, 2)
            vw = vimg.reshape(-1, 1, hd, wsz).transpose(0, 1, 3, 2)
            attn = jax.nn.softmax(part(q) * scale @ jnp.swapaxes(part(k), -1, -2), axis=-1)
            out = attn @ vw + lepe
            out = out.transpose(0, 2, 1, 3).reshape(B, nh, nw, H_sp, W_sp, C)
            out = out.transpose(0, 1, 3, 2, 4, 5).reshape(B, N, C)
            return out
        B, H, W = x.shape
        Hg, Wg = (H // 4, W // 4)
        C = DIM
        tok = x.reshape(B, H * W // C, C)
        qkv = (tok @ qkv_w).reshape(B, -1, 3, C)
        q, k, v = (qkv[:, :, 0], qkv[:, :, 1], qkv[:, :, 2])
        h = C // 2
        x1 = _branch(q[..., :h], k[..., :h], v[..., :h], conv_w0, conv_b0, 1, SPLIT, Hg, Wg)
        x2 = _branch(q[..., h:], k[..., h:], v[..., h:], conv_w1, conv_b1, SPLIT, 1, Hg, Wg)
        att = jnp.concatenate([x1, x2], axis=-1) @ proj_w + proj_b
        mu = att.mean(-1, keepdims=True)
        var = ((att - mu) ** 2).mean(-1, keepdims=True)
        normed = (att - mu) * lax.rsqrt(var + EPS) * ln_w + ln_b
        tok = tok + normed
        return jnp.transpose(tok, (0, 2, 1)).reshape(B, H, W)

    def _L0_ffn_ref(x, w_gate, w_up, w_down, s_gate, s_up, s_down):
        import jax, jax.numpy as jnp
        import numpy as np
        HIDDEN = 512
        INTER = 2048
        B, S = (4, 256)

        def _qmatmul(x, w_int8, scale):
            y = jnp.einsum('bsh,ho->bso', x, w_int8.astype(x.dtype))
            return y * scale
        gate = jax.nn.silu(_qmatmul(x, w_gate, s_gate))
        up = _qmatmul(x, w_up, s_up)
        fuse = gate * up
        return _qmatmul(fuse, w_down, s_down)
    x = L0_attn_x
    x = x + _layernorm(_L0_attn_ref(_layernorm(x, axis=-1), L0_attn_qkv_w, L0_attn_conv_w0, L0_attn_conv_b0, L0_attn_conv_w1, L0_attn_conv_b1, L0_attn_proj_w, L0_attn_proj_b, L0_attn_ln_w, L0_attn_ln_b), axis=-1)
    x = x + _layernorm(_L0_ffn_ref(_layernorm(x, axis=-1), L0_ffn_w_gate, L0_ffn_w_up, L0_ffn_w_down, L0_ffn_s_gate, L0_ffn_s_up, L0_ffn_s_down), axis=-1)
    return x

_drawn_inputs = setup_inputs


def setup_inputs(seed=0):
    import zlib

    import numpy as np

    out = dict(_drawn_inputs(seed))
    spreads = {'L0_attn_ln_w': (1.0, 0.2), 'L0_attn_ln_b': (0.0, 0.8)}
    factors = {'L0_attn_conv_b0': 5.989, 'L0_attn_conv_b1': 8.0, 'L0_attn_proj_b': 7.786}
    for name, (base, spread) in spreads.items():
        noise = np.random.default_rng([zlib.crc32(name.encode()), seed]).standard_normal(out[name].shape)
        drawn = base * np.exp(spread * noise) if base else spread * noise
        out[name] = jnp.asarray(drawn.astype(out[name].dtype))
    for name, factor in factors.items():
        out[name] = (out[name] * factor).astype(out[name].dtype)
    return out
```

```python
from contextlib import ExitStack

import concourse.bass as bass
from concourse import mybir

P = 128
B, H, W = 4, 1024, 512
C = 16
HB = C // 2
WIN = 8
INTER = 2048
EPS = 1e-5

ROWS = 512
TILES = B * H // ROWS
NCH = ROWS // (4 * WIN)
EDGE = W // 2
SLICES = 2
NQ = ROWS // P
KB = W // P
MB = INTER // P
QKVL = 4 * P
XSCALE = 2.0 ** 10
SOFTMAX_SCALE = HB ** -0.5

F32 = mybir.dt.float32
F16 = mybir.dt.float16
I8 = mybir.dt.int8
I32 = mybir.dt.int32
ALU = mybir.AluOpType
ACT = mybir.ActivationFunctionType
AX = mybir.AxisListType

UNITS = 4
CONSTS = 12
ATT_LINKS = 13


def sandwich_kernel(nc, x, qkv_w, conv_w0, conv_b0, conv_w1, conv_b1, proj_w, proj_b, ln_w, ln_b,
                    w_gate, w_up, w_down, s_gate, s_up, s_down, scratch, out):
    with ExitStack() as ctx:
        def sb(name, shape, dt=F32):
            return ctx.enter_context(nc.sbuf_tensor(name, shape, dt))

        def pb(name, shape=(P, 512), dt=F32):
            return ctx.enter_context(nc.psum_tensor(name, list(shape), dt))

        def sem(name):
            return ctx.enter_context(nc.semaphore(name))

        wg = sb("wg", [P, KB, INTER], F16)
        wu = sb("wu", [P, KB, INTER], F16)
        wd = sb("wd", [P, MB, W], F16)
        wqkvl = sb("wqkvl", [P, 4, WIN, C])
        wprev = sb("wprev", [P, WIN, HB])
        wnext = sb("wnext", [P, WIN, HB])
        wproj = sb("wproj", [P, P])
        ident = sb("ident", [P, P])
        pair = sb("pair", [P, P])
        bproj = sb("bproj", [P, C])
        lnw = sb("lnw", [P, C])
        lnb = sb("lnb", [P, C])
        neghalf = sb("neghalf", [P, WIN * WIN])
        eps1 = sb("eps1", [P, WIN])
        epsx = sb("epsx", [P, NQ])
        epsc = sb("epsc", [P, WIN * WIN])
        sgate = sb("sgate", [P, MB])
        sup = sb("sup", [P, MB])
        sdown = sb("sdown", [P, W])
        wsm = sb("wsm", [C, 3 * C])
        filt = sb("filt", [C, 2, HB * 9])
        wvt = sb("wvt", [C, 3, C])
        pws = sb("pws", [C, C])
        cbr = sb("cbr", [C, P])
        cbc = sb("cbc", [C, 1])
        pbias = sb("pbias", [P, C])
        msum = sb("msum", [P, 2])
        sprod = sb("sprod", [P, MB])
        top = sb("top", [P, 8])
        ones = sb("ones", [1, P])
        xb = sb("xb", [P, WIN, EDGE])
        bst = sb("bst", [P, WIN, 6])
        mv = sb("mv", [P, WIN, 2])
        dmean = sb("dmean", [P, WIN])
        ln1 = sb("ln1", [P, 4, WIN])
        xt = sb("xt", [P, WIN, P])
        qkvl = sb("qkvl", [P, SLICES, WIN, QKVL])
        xl = sb("xl", [P, SLICES, WIN, P])
        prod = sb("prod", [P, 2, 4 * WIN * WIN * HB])
        sum4 = sb("sum4", [P, 2, 1024])
        sum2 = sb("sum2", [P, 2, 512])
        probs = sb("probs", [P, 2, WIN, WIN, WIN])
        smax = sb("smax", [P, 2 * WIN * WIN])
        ssum = sb("ssum", [P, 2 * WIN * WIN])
        attn = sb("attn", [P, 2, WIN, WIN, HB])
        catt = sb("catt", [P, 2, 4, P])
        cent = sb("cent", [P, WIN, WIN, C])
        csq = catt[:].rearrange("p u h (t c) -> p (u h) t c", c=C)
        cvar = sb("cvar", [P, WIN * WIN])
        crs = sb("crs", [P, WIN * WIN])
        ratt = sb("ratt", [P, C, WIN, C])
        o1 = sb("o1", [P, NQ, W])
        xr = sb("xr", [P, NQ, W])
        x1 = sb("x1", [P, NQ, W])
        fst = sb("fst", [P, NQ, 6])
        fmv = sb("fmv", [P, 3, NQ, 2])
        frs = sb("frs", [P, 3, 2, NQ])
        yst = sb("yst", [P, NQ, 6])
        xhi = sb("xhi", [P, KB, ROWS], F16)
        xlo = sb("xlo", [P, KB, ROWS], F16)
        gact = sb("gact", [P, 2, ROWS])
        fuse = sb("fuse", [P, 2, ROWS])
        fhi = sb("fhi", [P, 2, ROWS], F16)
        flo = sb("flo", [P, 2, ROWS], F16)
        y = o1

        ps_gate = pb("ps_gate")
        ps_up = pb("ps_up")
        ps_acc = [pb(f"ps_acc{q}") for q in range(NQ)]
        ps_t = pb("ps_t")
        ps_q = pb("ps_q")

        s_const = sem("s_const")
        s_wload = [sem("s_wload_g"), sem("s_wload_u"), sem("s_wload_d")]
        s_blocks = sem("s_blocks")
        zeroed = sem("zeroed")
        wvt_done = sem("wvt_done")
        pws_done = sem("pws_done")
        cb_done = sem("cb_done")
        setup_dve = sem("setup_dve")
        bias_done = sem("bias_done")
        top_part = sem("top_part")
        top_row = sem("top_row")
        top_pow2 = sem("top_pow2")
        top_all = sem("top_all")
        scales_set = sem("scales_set")
        lnw_done = sem("lnw_done")
        ones_done = sem("ones_done")
        ident_done = sem("ident_done")
        setup_pool = sem("setup_pool")
        w_cast = sem("w_cast")
        t_read = sem("t_read")
        q_read = sem("q_read")
        s_xb = sem("s_xb")
        ln1_chain = sem("ln1_chain")
        ln1_stats = sem("ln1_stats")
        ln1_pair = sem("ln1_pair")
        ln1_var = sem("ln1_var")
        ln1_pool = sem("ln1_pool")
        ln1_rs = sem("ln1_rs")
        xn_done = sem("xn_done")
        xt_tr = sem("xt_tr")
        qkv_done = sem("qkv_done")
        xl_done = sem("xl_done")
        att_chain = sem("att_chain")
        prod_done = sem("prod_done")
        half_done = sem("half_done")
        sub_done = sem("sub_done")
        exp_done = sem("exp_done")
        cat_done = sem("cat_done")
        cat_tr = sem("cat_tr")
        proj_done = sem("proj_done")
        sq_done = sem("sq_done")
        cvar_done = sem("cvar_done")
        crs_chain = sem("crs_chain")
        crs_done = sem("crs_done")
        cn_done = sem("cn_done")
        ratt_done = sem("ratt_done")
        s_ratt = sem("s_ratt")
        s_o1 = sem("s_o1")
        s_xr = sem("s_xr")
        f_chain = sem("f_chain")
        f_stats = sem("f_stats")
        f_pool = sem("f_pool")
        f_rs = sem("f_rs")
        o1_norm = sem("o1_norm")
        xr_sum = sem("xr_sum")
        fx_done = sem("fx_done")
        fx_tr = sem("fx_tr")
        xhi_done = sem("xhi_done")
        gate_done = sem("gate_done")
        up_done = sem("up_done")
        silu_done = sem("silu_done")
        fuse_done = sem("fuse_done")
        fhi_done = sem("fhi_done")
        flo_done = sem("flo_done")
        down_done = sem("down_done")
        y_chain = sem("y_chain")
        acc_read = sem("acc_read")
        y_stats = sem("y_stats")
        y_pool = sem("y_pool")
        y_rs = sem("y_rs")
        y_norm = sem("y_norm")
        y_sum = sem("y_sum")
        x1_done = sem("x1_done")
        s_out = sem("s_out")

        x_att = x.rearrange("b (s k h a) (e w) -> (b s) e a k h w", s=2, k=NCH, h=WIN, a=4, e=2)
        x_ffn = x.rearrange("b (c s j) n -> b s c j n", c=C, s=2)
        out_ffn = out.rearrange("b (c s j) n -> b s c j n", c=C, s=2)
        r_store = scratch.rearrange("t k c (h a e w) -> t e a k (c h) w", h=WIN, a=4, e=2)
        r_load = scratch.rearrange("t k c (g f) -> t c k g f", g=2)

        def need(eng, s, value):
            if not (isinstance(value, int) and value <= 0):
                eng.wait_ge(s, value)

        USES = {"xt_transpose": (1, 0), "qkv": (0, 1), "cat_transpose": (1, 0), "proj": (0, 1),
                "ln1_fin": (0, 1), "fx_transpose": (1, 0)}

        def body_steps(first_half=True, ahead=True, ffn=True, prep=True):
            att = []
            if first_half:
                a = (1, 1)
                att += [("qk", a, 0), ("cat_transpose", (1, 0), 0), ("qk", a, 1), ("proj", (1, 0), 0),
                        ("cat_transpose", (1, 0), 1), ("qk", a, 2), ("proj", (1, 0), 1), ("qk", a, 3),
                        ("cent_var", (1, 0)), ("softmax", a), ("cent_out", (1, 0))]
                if ahead:
                    att += [("ln1_stats", 2)]
                att += [("pv", a, 0)]
                if ahead:
                    att += [("ln1_fin", 2)]
                att += [("pv", a, 1)]
                if ahead:
                    att += [("xt_transpose", (2, 0), 0), ("xt_transpose", (2, 0), 1)]
                att += [("pv", a, 2)]
                if ahead:
                    att += [("qkv", (2, 0), h) for h in range(0, 3)]
                att += [("pv", a, 3)]
                if ahead:
                    att += [("qkv", (2, 0), h) for h in range(3, 6)]
                att += [("attn_out", a)]
                if ahead:
                    att += [("qkv", (2, 0), h) for h in range(6, 8)]
                att += [("token_bias", (2, 0))] if ahead else []
                b = (2, 0)
                for i, step in enumerate([("cat_transpose", a, 0), ("proj", a, 0), ("cat_transpose", a, 1),
                                          ("proj", a, 1)]):
                    if ahead:
                        att += [("qk", b, i)]
                    att += [step]
                att += [("cent_var", a)]
                if ahead:
                    att += [("softmax", b)]
                att += [("cent_out", a), ("att_store", 1)]
                if ahead:
                    att += [("pv", b, 0), ("xt_transpose", (2, 1), 0), ("xt_transpose", (2, 1), 1), ("pv", b, 1)]
                    att += [("qkv", (2, 1), h) for h in range(0, 4)]
                    att += [("pv", b, 2)]
                    att += [("qkv", (2, 1), h) for h in range(4, 8)]
                    att += [("token_bias", (2, 1)), ("load_xb", 3)]
                att += [("ffn_norm1", 1)]
                if ahead:
                    att += [("pv", b, 3), ("attn_out", b)]
            tail = [("ffn_norm2", 1)] + [("fx_transpose", 1, k) for k in range(KB)] if first_half else []
            if not ffn:
                return att + tail + [("keep_x1", 1)]
            steps = []
            slots = 2 * MB
            done = 0
            for m in range(MB):
                for part in ("gate", "up"):
                    steps.append((part, 0, m))
                    upto = len(att) * (2 * m + (part == "up") + 1) // slots
                    steps += att[done:upto]
                    done = upto
                if m >= 1:
                    steps.append(("fuse_split", 0, m - 1))
                    steps.append(("down", 0, m - 1))
            steps.append(("fuse_split", 0, MB - 1))
            steps += tail
            steps.append(("down", 0, MB - 1))
            steps.append(("finish", 0))
            if first_half:
                steps.append(("keep_x1", 1))
            return steps

        START = [("load_xb", 0), ("ln1_stats", 0), ("ln1_fin", 0), ("xt_transpose", (0, 0), 0), ("xt_transpose", (0, 0), 1)] \
            + [("qkv", (0, 0), h) for h in range(8)] + [("token_bias", (0, 0))] \
            + [("xt_transpose", (0, 1), 0), ("xt_transpose", (0, 1), 1)] \
            + [("qk", (0, 0), 0), ("qk", (0, 0), 1)] \
            + [("qkv", (0, 1), h) for h in range(8)] + [("token_bias", (0, 1)), ("load_xb", 1)] \
            + [("qk", (0, 0), 2), ("qk", (0, 0), 3), ("softmax", (0, 0))] \
            + [("pv", (0, 0), u) for u in range(UNITS)] + [("attn_out", (0, 0))]
        BEFORE = body_steps(ffn=False)
        MIDDLE = body_steps()
        LAST2 = body_steps(ahead=False)
        LAST1 = body_steps(first_half=False, ahead=False)

        def uses(steps):
            return [sum(USES.get(s[0], (0, 0))[i] for s in steps) for i in (0, 1)]

        def walk(eng, todo):
            used = [0, 0]

            def run(steps, tile):
                for name, where, *rest in steps:
                    u = USES.get(name, (0, 0))
                    if name in todo:
                        at = tile + where if isinstance(where, int) else (tile + where[0], where[1])
                        skip = isinstance(tile, int) and name == "load_xb" and tile + where >= TILES
                        if not skip:
                            todo[name](at, *rest, used[0], used[1])
                    used[0] += u[0]
                    used[1] += u[1]

            run(START, 0)
            run(BEFORE, -1)
            run(MIDDLE, 0)
            n, before = uses(MIDDLE), list(used)
            with eng.Fori(1, TILES - 3) as t:
                used[:] = [before[i] + n[i] * (t - 1) for i in (0, 1)]
                run(MIDDLE, t)
            used[:] = [before[i] + n[i] * (TILES - 4) for i in (0, 1)]
            run(MIDDLE, TILES - 3)
            run(LAST2, TILES - 2)
            run(LAST1, TILES - 1)

        block = ctx.enter_context(nc.Block())

        @block.sync
        def _(sp):
            def load_xb(t, *_):
                need(sp, xt_tr, 4 * t)
                need(sp, xl_done, 4 * t)
                for e in range(2):
                    for a in range(4):
                        p0 = 64 * e + 16 * a
                        if isinstance(t, int):
                            src = x_att[t, e, a]
                        else:
                            src = x_att[bass.ds(t, 1), e, a].rearrange("o k h w -> (o k) h w")
                        sp.dma_start(xb[p0:p0 + NCH], src).then_inc(s_xb, 16)

            def att_store(t, *_):
                need(sp, ratt_done, 2 * t + 2)
                for e in range(2):
                    for a in range(4):
                        p0 = 64 * e + 16 * a
                        if isinstance(t, int):
                            dst = r_store[t, e, a]
                        else:
                            dst = r_store[bass.ds(t, 1), e, a].rearrange("o k s w -> (o k) s w")
                        sp.dma_start(dst, ratt[p0:p0 + NCH].rearrange("p c h w -> p (c h) w")).then_inc(s_ratt, 16)
                for q in range(NQ):
                    if q == 0:
                        need(sp, x1_done, t)
                    if q == 1:
                        need(sp, fx_tr, KB * t)
                    if q == 2:
                        need(sp, s_out, 64 * (t - 1))
                    if isinstance(t, int):
                        src = x_ffn[t // 2, t % 2, 4 * q:4 * q + 4]
                        sp.dma_start(xr[:, q, :], src).then_inc(s_xr, 16)
                    else:
                        src = x_ffn[bass.ds(t // 2, 1), bass.ds(t % 2, 1), 4 * q:4 * q + 4]
                        sp.dma_start(xr[:, q, :], src.rearrange("b s c j n -> (b s c) j n")).then_inc(s_xr, 16)
                if isinstance(t, int) and t == 0:
                    sp.wait_ge(w_cast, 3)
                sp.wait_ge(s_ratt, 128 * t + 128)
                for c in range(C):
                    src = r_load[t, c] if isinstance(t, int) else r_load[bass.ds(t, 1), c].rearrange("o k g f -> (o k) g f")
                    p0 = c % 4 * (P // 4)
                    sp.dma_start(o1[p0:p0 + P // 4, c // 4, :], src).then_inc(s_o1, 16)

            def finish(t, *_):
                for q in range(NQ):
                    sp.wait_ge(y_sum, NQ * t + q + 1)
                    if isinstance(t, int):
                        dst = out_ffn[t // 2, t % 2, 4 * q:4 * q + 4]
                    else:
                        dst = out_ffn[bass.ds(t // 2, 1), bass.ds(t % 2, 1), 4 * q:4 * q + 4]
                        dst = dst.rearrange("b s c j n -> (b s c) j n")
                    sp.dma_start(dst, y[:, q, :]).then_inc(s_out, 16)

            load_xb(0)
            sp.dma_start(wsm[:], qkv_w).then_inc(s_const, 16)
            for br, cw in ((0, conv_w0), (1, conv_w1)):
                flat = cw.rearrange("c o y x -> (c o y x)").rearrange("(o n) -> o n", o=1)
                sp.dma_start(filt[:, br, :], flat.broadcast_to([C, HB * 9])).then_inc(s_const, 16)
            sp.dma_start(pws[:], proj_w).then_inc(s_const, 16)
            sp.dma_start(cbc[0:HB, :], conv_b0.rearrange("(c o) -> c o", o=1),
                         allow_slow_non_contiguous=True).then_inc(s_const, 16)
            sp.dma_start(cbc[HB:C, :], conv_b1.rearrange("(c o) -> c o", o=1),
                         allow_slow_non_contiguous=True).then_inc(s_const, 16)
            for dst, src in ((pbias, proj_b), (lnw, ln_w), (lnb, ln_b), (sdown, s_down)):
                n = src.shape[0]
                sp.dma_start(dst[:], src.rearrange("(o n) -> o n", o=1).broadcast_to([P, n])).then_inc(s_const, 16)
            for dst, src in ((sgate, s_gate), (sup, s_up)):
                sp.dma_start(dst[:], src.rearrange("(m p) -> p m", p=P),
                             allow_slow_non_contiguous=True).then_inc(s_const, 16)
            sp.wait_ge(zeroed, 4)
            sp.wait_ge(wvt_done, 2)
            sp.wait_ge(s_const, 16 * CONSTS)
            for t in range(WIN):
                rows = slice(C * t, C * t + C)
                sp.dma_start(wqkvl[rows, 0:3, t, :], wsm[:].rearrange("p (g c) -> p g c", g=3)).then_inc(s_blocks, 16)
                sp.dma_start(wqkvl[rows, 3, t, :], wvt[:, 1, :]).then_inc(s_blocks, 16)
                if t + 1 < WIN:
                    sp.dma_start(wqkvl[rows, 3, t + 1, 0:HB], wvt[:, 0, 0:HB]).then_inc(s_blocks, 16)
                if t >= 1:
                    sp.dma_start(wqkvl[rows, 3, t - 1, 0:HB], wvt[:, 2, 0:HB]).then_inc(s_blocks, 16)
                sp.dma_start(wprev[rows, t, :], wvt[:, 0, HB:C]).then_inc(s_blocks, 16)
                sp.dma_start(wnext[rows, t, :], wvt[:, 2, HB:C]).then_inc(s_blocks, 16)
            sp.wait_ge(pws_done, 1)
            for t in range(WIN):
                sp.dma_start(wproj[C * t:C * t + C, C * t:C * t + C], pws[:]).then_inc(s_blocks, 16)
            sp.dma_start(prod[:, 0, :].bitcast(I32).rearrange("p (k n) -> p k n", k=KB),
                         w_gate.rearrange("(k p) n -> p k n", p=P)).then_inc(s_wload[0], 16)
            sp.dma_start(prod[:, 1, :].bitcast(I32).rearrange("p (k n) -> p k n", k=KB),
                         w_up.rearrange("(k p) n -> p k n", p=P)).then_inc(s_wload[1], 16)
            sp.dma_start(y[:].rearrange("p q n -> p (q n)").bitcast(I32).rearrange("p (m n) -> p m n", m=MB),
                         w_down.rearrange("(m p) n -> p m n", p=P)).then_inc(s_wload[2], 16)

            def load_later(t, *_):
                if not (isinstance(t, int) and t == 0):
                    load_xb(t)

            walk(sp, {"load_xb": load_later, "att_store": att_store, "finish": finish})
            sp.wait_ge(s_out, 64 * TILES)
            sp.wait_ge(s_ratt, 128 * TILES)

        BLOCKS = 16 * (6 * WIN - 2 + WIN)

        @block.tensor
        def _(pe):
            def ln1_fin(t, ut, uq):
                pe.wait_ge(ln1_stats, t + 1)
                need(pe, q_read, uq)
                nc.tensor.matmul(ps_q[:, 0:2 * WIN], pair[:], mv[:].rearrange("p h s -> p (h s)"),
                                 start=True, stop=True).then_inc(ln1_pair, 1)

            def xt_transpose(at, u, ut, uq):
                t, g = at
                pe.wait_ge(xn_done, t + 1)
                need(pe, t_read, ut)
                for i in range(4):
                    mm = nc.tensor.transpose(ps_t[:, P * i:P * i + P], xb[:, 4 * u + i, P * g:P * g + P], ident[:])
                mm.then_inc(xt_tr, 1)

            def qkv(at, h, ut, uq):
                t, g = at
                pe.wait_ge(t_read, ut)
                need(pe, q_read, uq)
                mm = nc.tensor.matmul(ps_q[:], xt[:, h, :], wqkvl[:].rearrange("p g t c -> p (g t c)"),
                                      start=True, stop=False, skip_group_check=True)
                down = ps_q[:, 3 * P:4 * P].rearrange("p (t c) -> p t c", t=WIN)[:, :, HB:C]
                if h >= 1:
                    mm = nc.tensor.matmul(down, xt[:, h - 1, :], wprev[:], start=False, stop=(h == WIN - 1),
                                          skip_group_check=True)
                if h + 1 < WIN:
                    mm = nc.tensor.matmul(down, xt[:, h + 1, :], wnext[:], start=False, stop=True,
                                          skip_group_check=True)
                mm.then_inc(qkv_done, 1)

            def cat_transpose(at, u, ut, uq):
                t, g = at
                pe.wait_ge(cat_done, 2 * t + g + 1)
                need(pe, t_read, ut)
                for i in range(4):
                    mm = nc.tensor.transpose(ps_t[:, P * i:P * i + P], qkvl[:, g, 4 * u + i, 3 * P:4 * P], ident[:])
                mm.then_inc(cat_tr, 1)

            def proj(at, u, ut, uq):
                pe.wait_ge(t_read, ut)
                need(pe, q_read, uq)
                for i in range(4):
                    mm = nc.tensor.matmul(ps_q[:, P * i:P * i + P], catt[:, u, i, :], wproj[:], start=True, stop=True)
                mm.then_inc(proj_done, 1)

            def fx_transpose(t, k, ut, uq):
                pe.wait_ge(fx_done, NQ * t + NQ)
                need(pe, t_read, ut)
                for q in range(NQ):
                    mm = nc.tensor.transpose(ps_t[:, P * q:P * q + P], o1[:, q, P * k:P * k + P], ident[:])
                mm.then_inc(fx_tr, 1)

            def gate_or_up(ps, w, done):
                for k in range(KB):
                    for part, xs in enumerate((xhi, xlo)):
                        mm = nc.tensor.matmul(ps[:], w[:, k, :], xs[:, k, :], start=(k == 0 and part == 0),
                                              stop=(k == KB - 1 and part == 1))
                mm.then_inc(done, 1)

            def gate(t, m, ut, uq):
                if m == 0:
                    pe.wait_ge(t_read, ut)
                need(pe, silu_done, MB * t + m)
                gate_or_up(ps_gate, wg[:, :, P * m:P * m + P], gate_done)

            def up(t, m, ut, uq):
                need(pe, fuse_done, MB * t + m)
                gate_or_up(ps_up, wu[:, :, P * m:P * m + P], up_done)

            def down(t, m, ut, uq):
                pe.wait_ge(flo_done, MB * t + m + 1)
                if m == 0:
                    need(pe, acc_read, NQ * t)
                for part, f in enumerate((fhi, flo)):
                    for q in range(NQ):
                        mm = nc.tensor.matmul(ps_acc[q][:], f[:, m % 2, P * q:P * q + P], wd[:, m, :],
                                              start=(m == 0 and part == 0), stop=(m == MB - 1 and part == 1))
                mm.then_inc(down_done, 1)

            pe.wait_ge(ident_done, 2)
            pe.wait_ge(pws_done, 1)
            pe.wait_ge(cb_done, 1)
            nc.tensor.matmul(ps_up[:, 0:C], cbr[:], pws[:], start=True, stop=True).then_inc(bias_done, 1)
            pe.wait_ge(top_part, 1)
            nc.tensor.transpose(ps_gate[0:1, 0:P], top[:, 0:1], ident[:]).then_inc(top_row, 1)
            pe.wait_ge(top_pow2, 1)
            pe.wait_ge(ones_done, 1)
            nc.tensor.matmul(ps_acc[0][:, 0:1], ones[:], top[0:1, 2:3], start=True, stop=True).then_inc(top_all, 1)
            pe.wait_ge(s_blocks, BLOCKS)
            todo = {"ln1_fin": ln1_fin, "xt_transpose": xt_transpose, "qkv": qkv, "cat_transpose": cat_transpose,
                    "proj": proj, "fx_transpose": fx_transpose, "gate": gate, "up": up, "down": down}

            def first_gate(t, m, ut, uq):
                if isinstance(t, int) and t == 0 and m == 0:
                    pe.wait_ge(w_cast, 3)
                gate(t, m, ut, uq)

            todo["gate"] = first_gate
            walk(pe, todo)

        @block.scalar
        def _(act):
            def ln1_fin(t, ut, uq):
                act.wait_ge(ln1_rs, t + 1)
                for h in range(WIN):
                    a = nc.scalar.activation(xb[:, h, :], xb[:, h, :], ACT.Identity, bias=ln1[:, 3, h:h + 1],
                                             scale=ln1[:, 2, h:h + 1])
                a.then_inc(xn_done, 1)

            def xt_transpose(at, u, ut, uq):
                t, g = at
                act.wait_ge(xt_tr, 4 * t + 2 * g + u + 1)
                nc.scalar.activation(xt[:, 4 * u:4 * u + 4, :].rearrange("p h r -> p (h r)"), ps_t[:],
                                     ACT.Copy).then_inc(t_read, 1)

            def qkv(at, h, ut, uq):
                t, g = at
                act.wait_ge(qkv_done, WIN * (2 * t + g) + h + 1)
                if h == 0:
                    need(act, cat_tr, 2 * (2 * t + g) - 2)
                nc.scalar.activation(qkvl[:, g, h, :], ps_q[:], ACT.Copy).then_inc(q_read, 1)

            def softmax(at, ut, uq):
                t, g = at
                act.wait_ge(sub_done, 2 * t + g + 1)
                pr = probs[:].rearrange("p b w i j -> p (b w i j)")
                nc.scalar.activation(pr, pr, ACT.Exp, scale=SOFTMAX_SCALE).then_inc(exp_done, 1)

            def cat_transpose(at, u, ut, uq):
                t, g = at
                act.wait_ge(cat_tr, 2 * (2 * t + g) + u + 1)
                need(act, cvar_done, 2 * t + g)
                nc.scalar.activation(catt[:, u].rearrange("p h r -> p (h r)"), ps_t[:], ACT.Copy).then_inc(t_read, 1)

            def proj(at, u, ut, uq):
                act.wait_ge(q_read, uq + 1)
                part = slice(4 * u, 4 * u + 4)
                nc.scalar.activation(csq[:, part].rearrange("p h t c -> p (h t c)"),
                                     cent[:, part].rearrange("p h t c -> p (h t c)"), ACT.Square).then_inc(sq_done, 1)

            def ffn_norm1(t, ut, uq):
                act.wait_ge(f_rs, 2 * t + 1)
                for q in range(NQ):
                    nc.scalar.activation(o1[:, q, :], o1[:, q, :], ACT.Identity, bias=frs[:, 0, 1, q:q + 1],
                                         scale=frs[:, 0, 0, q:q + 1]).then_inc(o1_norm, 1)

            def ffn_norm2(t, ut, uq):
                act.wait_ge(f_rs, 2 * t + 2)
                for q in range(NQ):
                    nc.scalar.activation(o1[:, q, :], xr[:, q, :], ACT.Identity, bias=frs[:, 1, 1, q:q + 1],
                                         scale=frs[:, 1, 0, q:q + 1]).then_inc(fx_done, 1)

            def fx_transpose(t, k, ut, uq):
                act.wait_ge(fx_tr, KB * t + k + 1)
                nc.scalar.activation(xhi[:, k, :], ps_t[:], ACT.Copy).then_inc(xhi_done, 1)

            def gate(t, m, ut, uq):
                act.wait_ge(gate_done, MB * t + m + 1)
                need(act, fuse_done, MB * t + m - 1)
                nc.scalar.activation(gact[:, m % 2, :], ps_gate[:], ACT.Silu,
                                     scale=sgate[:, m:m + 1]).then_inc(silu_done, 1)

            def fuse_split(t, m, ut, uq):
                act.wait_ge(fuse_done, MB * t + m + 1)
                need(act, down_done, MB * t + m - 1)
                nc.scalar.activation(fhi[:, m % 2, :], fuse[:, m % 2, :], ACT.Copy).then_inc(fhi_done, 1)

            def finish(t, ut, uq):
                act.wait_ge(y_rs, t + 1)
                for q in range(NQ):
                    nc.scalar.activation(y[:, q, :], y[:, q, :], ACT.Identity, bias=frs[:, 2, 1, q:q + 1],
                                         scale=frs[:, 2, 0, q:q + 1]).then_inc(y_norm, 1)

            def keep_x1(t, ut, uq):
                need(act, y_sum, NQ * t)
                nc.scalar.activation(x1[:], xr[:], ACT.Copy).then_inc(x1_done, 1)

            act.wait_ge(scales_set, 1)
            walk(act, {"ln1_fin": ln1_fin, "xt_transpose": xt_transpose, "qkv": qkv, "softmax": softmax,
                       "cat_transpose": cat_transpose, "proj": proj, "ffn_norm1": ffn_norm1,
                       "ffn_norm2": ffn_norm2, "fx_transpose": fx_transpose, "gate": gate,
                       "fuse_split": fuse_split, "finish": finish, "keep_x1": keep_x1})

        @block.gpsimd
        def _(pool):
            def inv_std(rs, nb, var, negmean, eps, chain, base, done):
                n = rs.shape[1]
                nc.gpsimd.tensor_tensor(rs, var, eps[:, 0:n], ALU.add).then_inc(chain, 1)
                pool.wait_ge(chain, base + 1)
                nc.gpsimd.tensor_tensor(rs, rs, neghalf[:, 0:n], ALU.pow).then_inc(chain, 1)
                pool.wait_ge(chain, base + 2)
                nc.gpsimd.tensor_tensor(nb, negmean, rs, ALU.mult).then_inc(done, 1)

            def ln1_fin(t, ut, uq):
                pool.wait_ge(ln1_var, t + 1)
                pool.wait_ge(q_read, uq + 1)
                inv_std(ln1[:, 2, :], ln1[:, 3, :], ln1[:, 0, :], ln1[:, 1, :], eps1, ln1_pool, 2 * t, ln1_rs)

            def token_bias(at, ut, uq):
                t, g = at
                pool.wait_ge(xn_done, t + 1)
                need(pool, ratt_done, 2 * t + g - 1)
                src = xb[:, :, P * g:P * g + P].rearrange("p h (t c) -> p h t c", c=C)
                dst = xl[:, g].rearrange("p h (t c) -> p (h t) c", c=C)
                nc.gpsimd.tensor_tensor(xl[:, g].rearrange("p h (t c) -> p h t c", c=C), src,
                                        lnb[:, None, None, :].broadcast_to([P, WIN, WIN, C]),
                                        ALU.add).then_inc(xl_done, 2)

            def halve(n, u, stage):
                pool.wait_ge(prod_done, 2 * UNITS * n + UNITS * stage + u + 1)
                return prod[:, u % 2, :], sum4[:, u % 2, :]

            def sum4_free(n, u, stage):
                links = [1, 2, 3, 4, 8, 9, 10, 11]
                i = UNITS * stage + u - 2
                need(pool, att_chain, ATT_LINKS * n + links[i] if i >= 0 else ATT_LINKS * (n - 1) + links[i])

            def qk(at, u, ut, uq):
                t, g = at
                n = 2 * t + g
                src, dst = halve(n, u, 0)
                sum4_free(n, u, 0)
                s = src.rearrange("p (s c) -> p s c", c=HB)
                nc.gpsimd.tensor_tensor(dst.rearrange("p (s c) -> p s c", c=4), s[:, :, 0:4], s[:, :, 4:8],
                                        ALU.add).then_inc(half_done, 1)

            def pv(at, u, ut, uq):
                t, g = at
                n = 2 * t + g
                src, dst = halve(n, u, 1)
                sum4_free(n, u, 1)
                s = src.rearrange("p (w jc) -> p w jc", jc=WIN * HB)
                nc.gpsimd.tensor_tensor(dst.rearrange("p (w jc) -> p w jc", jc=4 * HB), s[:, :, 0:4 * HB],
                                        s[:, :, 4 * HB:], ALU.add).then_inc(half_done, 1)

            def cent_var(at, ut, uq):
                t, g = at
                n = 2 * t + g
                pool.wait_ge(cvar_done, n + 1)
                need(pool, cn_done, n)
                nc.gpsimd.tensor_tensor(crs[:], cvar[:], epsc[:], ALU.add).then_inc(crs_chain, 1)
                pool.wait_ge(crs_chain, 2 * n + 1)
                nc.gpsimd.tensor_tensor(crs[:], crs[:], neghalf[:], ALU.pow).then_inc(crs_done, 1)

            def cent_out(at, ut, uq):
                t, g = at
                n = 2 * t + g
                pool.wait_ge(cn_done, n + 1)
                nc.gpsimd.tensor_tensor(cent[:].rearrange("p h t c -> p (h t) c"),
                                        cent[:].rearrange("p h t c -> p (h t) c"),
                                        lnw[:, None, :].broadcast_to([P, WIN * WIN, C]), ALU.mult).then_inc(crs_chain, 1)
                pool.wait_ge(crs_chain, 2 * n + 2)
                pool.wait_ge(xl_done, 2 * n + 2)
                if g == 0:
                    need(pool, s_ratt, 128 * t)
                nc.gpsimd.tensor_tensor(ratt[:, :, :, WIN * g:WIN * g + WIN].rearrange("p c h t -> p h t c"),
                                        cent[:], xl[:, g].rearrange("p h (t c) -> p h t c", c=C),
                                        ALU.add).then_inc(ratt_done, 1)

            def ffn_norm1(t, ut, uq):
                pool.wait_ge(f_stats, 2 * t + 1)
                inv_std(frs[:, 0, 0, :], frs[:, 0, 1, :], fmv[:, 0, :, 1], fmv[:, 0, :, 0], eps1, f_pool, 4 * t, f_rs)
                pool.wait_ge(s_xr, 64 * t + 64)
                for q in range(NQ):
                    pool.wait_ge(o1_norm, NQ * t + q + 1)
                    nc.gpsimd.tensor_tensor(xr[:, q, :], xr[:, q, :], o1[:, q, :], ALU.add).then_inc(xr_sum, 1)

            def ffn_norm2(t, ut, uq):
                pool.wait_ge(f_stats, 2 * t + 2)
                inv_std(frs[:, 1, 0, :], frs[:, 1, 1, :], fmv[:, 1, :, 1], fmv[:, 1, :, 0], epsx, f_pool, 4 * t + 2,
                        f_rs)

            def finish(t, ut, uq):
                pool.wait_ge(y_stats, t + 1)
                inv_std(frs[:, 2, 0, :], frs[:, 2, 1, :], fmv[:, 2, :, 1], fmv[:, 2, :, 0], eps1, y_pool, 2 * t, y_rs)
                pool.wait_ge(x1_done, t + 1)
                for q in range(NQ):
                    pool.wait_ge(y_norm, NQ * t + q + 1)
                    nc.gpsimd.tensor_tensor(y[:, q, :], y[:, q, :], x1[:, q, :], ALU.add).then_inc(y_sum, 1)

            nc.gpsimd.memset(ident[:], 0.0).then_inc(setup_pool, 1)
            nc.gpsimd.memset(pair[:], 0.0).then_inc(setup_pool, 1)
            for const, value in ((neghalf, -0.5), (eps1, EPS), (epsx, EPS * XSCALE ** -2), (epsc, EPS * C)):
                nc.gpsimd.memset(const[:], value).then_inc(setup_pool, 1)
            pool.wait_ge(setup_pool, 6)
            nc.gpsimd.affine_select(out=ident[:], in_=ident[:], compare_op=ALU.not_equal, fill=1.0, base=0,
                                    pattern=[[-1, P]], channel_multiplier=1).then_inc(ident_done, 1)
            for i, off in enumerate((0, 64, -64)):
                if i:
                    pool.wait_ge(setup_pool, 6 + i)
                a = nc.gpsimd.affine_select(out=pair[:], in_=pair[:], compare_op=ALU.not_equal, fill=0.5, base=off,
                                            pattern=[[-1, P]], channel_multiplier=1)
                a.then_inc(ident_done if i == 2 else setup_pool, 1)
            for i, (dst, src) in enumerate((
                    (wg[:].rearrange("p k n -> p (k n)"), prod[:, 0, :].bitcast(I8)),
                    (wu[:].rearrange("p k n -> p (k n)"), prod[:, 1, :].bitcast(I8)),
                    (wd[:].rearrange("p m n -> p (m n)"), y[:].rearrange("p q n -> p (q n)").bitcast(I8)))):
                pool.wait_ge(s_wload[i], 16)
                nc.gpsimd.tensor_copy(dst, src).then_inc(w_cast, 1)

            pool.wait_ge(s_const, 16 * CONSTS)
            pool.wait_ge(lnw_done, 1)
            walk(pool, {"ln1_fin": ln1_fin, "token_bias": token_bias, "qk": qk, "pv": pv, "cent_var": cent_var,
                        "cent_out": cent_out, "ffn_norm1": ffn_norm1, "ffn_norm2": ffn_norm2, "finish": finish})

        @block.vector
        def _(dve):
            def mean_var(st, n, mean, var, chain, base, done, sign, scale=1.0):
                dve.wait_ge(chain, base + 1)
                nc.vector.tensor_tensor(mean, st[:, :, 1], st[:, :, 4], ALU.add)
                nc.vector.tensor_tensor(st[:, :, 0], st[:, :, 1], st[:, :, 4], ALU.subtract)
                nc.vector.tensor_tensor(st[:, :, 3], st[:, :, 2], st[:, :, 5], ALU.add).then_inc(chain, 1)
                dve.wait_ge(chain, base + 2)
                nc.vector.tensor_scalar(mean, mean, 0.5 * sign, None, ALU.mult)
                nc.vector.scalar_tensor_tensor(st[:, :, 0], st[:, :, 0], 0.25 * scale, st[:, :, 0], ALU.mult,
                                               ALU.mult).then_inc(chain, 1)
                dve.wait_ge(chain, base + 3)
                nc.vector.scalar_tensor_tensor(var, st[:, :, 3], scale / n, st[:, :, 0], ALU.mult,
                                               ALU.add).then_inc(done, 1)

            def ln1_stats_(t, ut, uq):
                dve.wait_ge(s_xb, 128 * t + 128)
                for h in range(WIN):
                    a = nc.vector.bn_stats(bst[:, h, :], xb[:, h, :])
                a.then_inc(ln1_chain, 1)
                mean_var(bst, EDGE, mv[:, :, 0], mv[:, :, 1], ln1_chain, 5 * t, ln1_stats, 1.0)

            def ln1_fin(t, ut, uq):
                dve.wait_ge(ln1_pair, t + 1)
                avg = ps_q[:, 0:2 * WIN].rearrange("p (h s) -> p h s", s=2)
                nc.vector.tensor_tensor(dmean[:], mv[:, :, 0], avg[:, :, 0], ALU.subtract).then_inc(ln1_chain, 1)
                dve.wait_ge(ln1_chain, 5 * t + 4)
                nc.vector.tensor_tensor(dmean[:], dmean[:], dmean[:], ALU.mult).then_inc(ln1_chain, 1)
                dve.wait_ge(ln1_chain, 5 * t + 5)
                nc.vector.tensor_tensor(ln1[:, 0, :], dmean[:], avg[:, :, 1], ALU.add).then_inc(ln1_var, 1)
                nc.vector.tensor_scalar(ln1[:, 1, :], avg[:, :, 0], -1.0, None, ALU.mult).then_inc(q_read, 1)

            def window(g, part, br, w):
                v = qkvl[:, g, :, P * part:P * part + P].rearrange("p h (t c) -> p h t c", c=C)
                return v[:, w, :, 0:HB] if br == 0 else v[:, :, w, HB:C]

            def products(at, u, stage, left, right):
                t, g = at
                n = 2 * t + g
                need(dve, half_done, 2 * UNITS * n + UNITS * stage + u - 1)
                for i in range(4):
                    br, w = u // 2, 4 * (u % 2) + i
                    dst = prod[:, u % 2, 512 * i:512 * i + 512].rearrange("p (i j c) -> p i j c", i=WIN, j=WIN)
                    a = nc.vector.tensor_tensor(dst, left(g, br, w), right(g, br, w), ALU.mult)
                a.then_inc(prod_done, 1)

            def reduce_unit(at, u, stage, dst):
                t, g = at
                n = 2 * t + g
                dve.wait_ge(half_done, 2 * UNITS * n + UNITS * stage + u + 1)
                link = ATT_LINKS * n + 7 * stage + u + 1
                if stage == 0:
                    a = sum4[:, u % 2, :].rearrange("p (s c) -> p s c", c=4)
                    b = sum2[:, u % 2, :].rearrange("p (s c) -> p s c", c=2)
                    nc.vector.tensor_tensor(b, a[:, :, 0:2], a[:, :, 2:4], ALU.add).then_inc(att_chain, 1)
                    dve.wait_ge(att_chain, link)
                    return nc.vector.tensor_tensor(dst, b[:, :, 0], b[:, :, 1], ALU.add)
                a = sum4[:, u % 2, :].rearrange("p (w jc) -> p w jc", jc=4 * HB)
                b = sum2[:, u % 2, :].rearrange("p (w jc) -> p w jc", jc=2 * HB)
                nc.vector.tensor_tensor(b, a[:, :, 0:2 * HB], a[:, :, 2 * HB:], ALU.add).then_inc(att_chain, 1)
                dve.wait_ge(att_chain, link)
                return nc.vector.tensor_tensor(dst, b[:, :, 0:HB], b[:, :, HB:], ALU.add)

            def scores_at(u):
                return probs[:, u // 2, 4 * (u % 2):4 * (u % 2) + 4].rearrange("p w i j -> p (w i j)")

            def attn_at(u):
                return attn[:, u // 2, 4 * (u % 2):4 * (u % 2) + 4].rearrange("p w i c -> p (w i) c")

            def qk(at, u, ut, uq):
                t, g = at
                if u == 0:
                    dve.wait_ge(q_read, uq)
                if u == 0 and isinstance(t, int) and 2 * t + g == 0:
                    dve.wait_ge(w_cast, 2)
                products(at, u, 0,
                         lambda g, br, w: window(g, 0, br, w)[:, :, None, :].broadcast_to([P, WIN, WIN, HB]),
                         lambda g, br, w: window(g, 1, br, w)[:, None, :, :].broadcast_to([P, WIN, WIN, HB]))
                if u >= 1:
                    reduce_unit(at, u - 1, 0, scores_at(u - 1))

            def softmax(at, ut, uq):
                t, g = at
                n = 2 * t + g
                reduce_unit(at, UNITS - 1, 0, scores_at(UNITS - 1)).then_inc(att_chain, 1)
                dve.wait_ge(att_chain, ATT_LINKS * n + 5)
                pr = probs[:].rearrange("p b w i j -> p (b w i) j")
                nc.vector.tensor_reduce(smax[:], pr, AX.X, ALU.max).then_inc(att_chain, 1)
                dve.wait_ge(att_chain, ATT_LINKS * n + 6)
                nc.vector.tensor_tensor(pr, pr, smax[:, :, None].broadcast_to([P, 2 * WIN * WIN, WIN]),
                                        ALU.subtract).then_inc(sub_done, 1)

            def pv(at, u, ut, uq):
                t, g = at
                n = 2 * t + g
                if u == 0:
                    dve.wait_ge(exp_done, n + 1)
                products(at, u, 1,
                         lambda g, br, w: probs[:, br, w][:, :, :, None].broadcast_to([P, WIN, WIN, HB]),
                         lambda g, br, w: window(g, 2, br, w)[:, None, :, :].broadcast_to([P, WIN, WIN, HB]))
                if u == 1:
                    nc.vector.tensor_reduce(ssum[:], probs[:].rearrange("p b w i j -> p (b w i) j"), AX.X,
                                            ALU.add).then_inc(att_chain, 1)
                    dve.wait_ge(att_chain, ATT_LINKS * n + 7)
                    nc.vector.reciprocal(ssum[:], ssum[:])
                if u >= 1:
                    reduce_unit(at, u - 1, 1, attn_at(u - 1))

            def attn_out(at, ut, uq):
                t, g = at
                n = 2 * t + g
                reduce_unit(at, UNITS - 1, 1, attn_at(UNITS - 1)).then_inc(att_chain, 1)
                dve.wait_ge(att_chain, ATT_LINKS * n + 12)
                o = attn[:].rearrange("p b w i c -> p (b w i) c")
                nc.vector.tensor_tensor(o, o, ssum[:, :, None].broadcast_to([P, 2 * WIN * WIN, HB]),
                                        ALU.mult).then_inc(att_chain, 1)
                dve.wait_ge(att_chain, ATT_LINKS * n + 13)
                cat = qkvl[:, g, :, 3 * P:4 * P].rearrange("p h (t c) -> p h t c", c=C)
                nc.vector.tensor_tensor(cat[:, :, :, 0:HB], cat[:, :, :, 0:HB], attn[:, 0], ALU.add)
                cat1 = cat[:, :, :, HB:C].rearrange("p h t c -> p t h c")
                nc.vector.tensor_tensor(cat1, cat1, attn[:, 1], ALU.add).then_inc(cat_done, 1)

            def proj(at, u, ut, uq):
                t, g = at
                dve.wait_ge(proj_done, 2 * (2 * t + g) + u + 1)
                need(dve, ratt_done, 2 * t + g)
                nc.vector.tensor_tensor(cent[:, 4 * u:4 * u + 4].rearrange("p h t c -> p (h t) c"),
                                        ps_q[:].rearrange("p (s c) -> p s c", c=C),
                                        bproj[:, None, :].broadcast_to([P, 4 * WIN, C]), ALU.add).then_inc(q_read, 1)

            def cent_var(at, ut, uq):
                t, g = at
                dve.wait_ge(sq_done, 2 * (2 * t + g) + 2)
                nc.vector.tensor_reduce(cvar[:], csq.rearrange("p h t c -> p (h t) c"), AX.X,
                                        ALU.add).then_inc(cvar_done, 1)

            def cent_out(at, ut, uq):
                t, g = at
                dve.wait_ge(crs_done, 2 * t + g + 1)
                c = cent[:].rearrange("p h t c -> p (h t) c")
                nc.vector.tensor_tensor(c, c, crs[:, :, None].broadcast_to([P, WIN * WIN, C]),
                                        ALU.mult).then_inc(cn_done, 1)

            def row_stats(src, i, st, chain, base, done, scale=1.0):
                for q in range(NQ):
                    a = nc.vector.bn_stats(st[:, q, :], src[:, q, :])
                a.then_inc(chain, 1)
                mean_var(st, W, fmv[:, i, :, 0], fmv[:, i, :, 1], chain, base, done, -1.0, scale)

            def ffn_norm1(t, ut, uq):
                dve.wait_ge(s_o1, 16 * C * (t + 1))
                row_stats(o1, 0, fst, f_chain, 6 * t, f_stats)

            def ffn_norm2(t, ut, uq):
                dve.wait_ge(xr_sum, NQ * t + NQ)
                row_stats(xr, 1, fst, f_chain, 6 * t + 3, f_stats, XSCALE ** -2)

            def fx_transpose(t, k, ut, uq):
                dve.wait_ge(xhi_done, KB * t + k + 1)
                nc.vector.tensor_tensor(xlo[:, k, :], ps_t[:], xhi[:, k, :], ALU.subtract).then_inc(t_read, 1)

            def up(t, m, ut, uq):
                dve.wait_ge(up_done, MB * t + m + 1)
                dve.wait_ge(silu_done, MB * t + m + 1)
                need(dve, flo_done, MB * t + m - 1)
                nc.vector.scalar_tensor_tensor(fuse[:, m % 2, :], ps_up[:], sup[:, m:m + 1], gact[:, m % 2, :],
                                               ALU.mult, ALU.mult).then_inc(fuse_done, 1)

            def fuse_split(t, m, ut, uq):
                dve.wait_ge(fhi_done, MB * t + m + 1)
                nc.vector.tensor_tensor(flo[:, m % 2, :], fuse[:, m % 2, :], fhi[:, m % 2, :],
                                        ALU.subtract).then_inc(flo_done, 1)

            def finish(t, ut, uq):
                dve.wait_ge(down_done, MB * t + MB)
                if not (isinstance(t, int) and t == TILES - 1):
                    dve.wait_ge(fx_tr, KB * (t + 2))
                else:
                    dve.wait_ge(s_out, 64 * t)
                for q in range(NQ):
                    nc.vector.tensor_tensor(y[:, q, :], ps_acc[q][:], sdown[:], ALU.mult).then_inc(acc_read, 1)
                dve.wait_ge(acc_read, NQ * t + NQ)
                row_stats(y, 2, yst, y_chain, 3 * t, y_stats)

            for wz in (wqkvl, wprev, wnext, wproj):
                nc.vector.memset(wz[:], 0.0).then_inc(zeroed, 1)
            nc.vector.memset(ones[:], 1.0).then_inc(ones_done, 1)
            steps = [0]

            def link(ins):
                steps[0] += 1
                ins.then_inc(setup_dve, 1)
                dve.wait_ge(setup_dve, steps[0])

            dve.wait_ge(s_const, 16 * CONSTS)
            for br in range(2):
                f = filt[:, br, :].rearrange("p (c f) -> p f c", f=9)
                part = slice(HB * br, HB * br + HB)
                nc.vector.tensor_tensor(wvt[:, :, part],
                                        wsm[:, None, 2 * C + HB * br:2 * C + HB * br + HB].broadcast_to([C, 3, HB]),
                                        f[:, 3:6, :] if br == 0 else f[:, 1:8:3, :], ALU.mult).then_inc(wvt_done, 1)
            for mat, mean, done in ((pws, msum[0:C, 0:1], pws_done), (pbias, msum[:, 1:2], setup_dve)):
                link(nc.vector.tensor_reduce(mean, mat[:], AX.X, ALU.add))
                link(nc.vector.tensor_scalar(mean, mean, 1.0 / C, None, ALU.mult))
                if mat is pws:
                    nc.vector.tensor_scalar(mat[:], mat[:], mean, None, ALU.subtract).then_inc(done, 1)
                else:
                    link(nc.vector.tensor_scalar(mat[:], mat[:], mean, None, ALU.subtract))
            nc.vector.tensor_copy(cbr[:], cbc[:].broadcast_to([C, P])).then_inc(cb_done, 1)
            nc.vector.tensor_scalar(lnw[:], lnw[:], C ** 0.5, None, ALU.mult).then_inc(lnw_done, 1)
            link(nc.vector.tensor_tensor(sprod[:], sgate[:], sup[:], ALU.mult))
            nc.vector.tensor_reduce(top[:, 0:1], sprod[:], AX.X, ALU.max, apply_absolute_value=True).then_inc(top_part, 1)
            dve.wait_ge(top_row, 1)
            link(nc.vector.tensor_reduce(top[0:1, 1:2], ps_gate[0:1, 0:P], AX.X, ALU.max))
            link(nc.vector.tensor_scalar(top[0:1, 1:2], top[0:1, 1:2], 2.0 ** -90, None, ALU.max))
            nc.vector.tensor_scalar(top[0:1, 2:3].bitcast(I32), top[0:1, 1:2].bitcast(I32), 0x7F800000, None,
                                    ALU.bitwise_and).then_inc(top_pow2, 1)
            dve.wait_ge(top_all, 1)
            link(nc.vector.tensor_copy(top[:, 3:4], ps_acc[0][:, 0:1]))
            link(nc.vector.reciprocal(top[:, 4:5], top[:, 3:4]))
            nc.vector.tensor_scalar(sup[:], sup[:], top[:, 4:5], 2.0 ** -18 / XSCALE, ALU.mult, ALU.mult)
            nc.vector.tensor_scalar(sdown[:], sdown[:], top[:, 3:4], 2.0 ** 18, ALU.mult, ALU.mult)
            nc.vector.tensor_scalar(sgate[:], sgate[:], 1.0 / XSCALE, None, ALU.mult)
            dve.wait_ge(bias_done, 1)
            nc.vector.tensor_tensor(bproj[:], pbias[:], ps_up[:, 0:C], ALU.add).then_inc(scales_set, 1)
            dve.wait_ge(scales_set, 1)

            walk(dve, {"ln1_stats": ln1_stats_, "ln1_fin": ln1_fin, "qk": qk, "softmax": softmax, "pv": pv,
                       "attn_out": attn_out, "proj": proj, "cent_var": cent_var, "cent_out": cent_out,
                       "ffn_norm1": ffn_norm1, "ffn_norm2": ffn_norm2, "fx_transpose": fx_transpose, "up": up,
                       "fuse_split": fuse_split, "finish": finish})


_INS = ["L0_attn_x", "L0_attn_qkv_w", "L0_attn_conv_w0", "L0_attn_conv_b0", "L0_attn_conv_w1", "L0_attn_conv_b1",
        "L0_attn_proj_w", "L0_attn_proj_b", "L0_attn_ln_w", "L0_attn_ln_b", "L0_ffn_w_gate", "L0_ffn_w_up",
        "L0_ffn_w_down", "L0_ffn_s_gate", "L0_ffn_s_up", "L0_ffn_s_down"]


def kernel(**inputs):
    import numpy as _np
    import concourse.bacc as _bacc
    from concourse import mybir as _mybir
    from concourse.bass_utils import run_bass_kernel_spmd as _run

    nc = _bacc.Bacc("TRN2", target_bir_lowering=False, num_devices=1)
    arrays, args = {}, []
    for name in _INS:
        a = _np.ascontiguousarray(inputs[name])
        if a.dtype == _np.int8:
            a = a.view(_np.int32)
        arrays[f"in_{name}"] = a
        args.append(nc.dram_tensor(f"in_{name}", a.shape, _mybir.dt.from_np(a.dtype), kind="ExternalInput").ap())
    scratch = nc.dram_tensor("attn_rows", (TILES, NCH, C, 2 * W), F32, kind="Internal").ap()
    out = nc.dram_tensor("out_x", (B, H, W), F32, kind="ExternalOutput").ap()
    sandwich_kernel(nc, *args, scratch, out)
    r = _run(nc, [arrays], core_ids=[0])
    return r.results[0]["out_x"]
```

```python
from contextlib import ExitStack

import concourse.bass as bass
from concourse import mybir

P = 128
B, H, W = 4, 1024, 512
C = 16
HB = C // 2
WIN = 8
INTER = 2048
EPS = 1e-5

ROWS = 512
TILES = B * H // ROWS
NCH = ROWS // (4 * WIN)
EDGE = W // 2
SLICES = 2
NQ = ROWS // P
KB = W // P
MB = INTER // P
QKVL = 4 * P
XSCALE = 2.0 ** 10
SOFTMAX_SCALE = HB ** -0.5

F32 = mybir.dt.float32
F16 = mybir.dt.float16
I8 = mybir.dt.int8
I32 = mybir.dt.int32
ALU = mybir.AluOpType
ACT = mybir.ActivationFunctionType
AX = mybir.AxisListType

UNITS = 4
FIRST_CONSTS = 3
LATER = 9
CASTS = 3 * KB
SETUP_POOL = 5
ATT_LINKS = 13


def sandwich_kernel(nc, x, qkv_w, conv_w0, conv_b0, conv_w1, conv_b1, proj_w, proj_b, ln_w, ln_b,
                    w_gate, w_up, w_down, s_gate, s_up, s_down, scratch, out):
    with ExitStack() as ctx:
        def sb(name, shape, dt=F32):
            return ctx.enter_context(nc.sbuf_tensor(name, shape, dt))

        def pb(name, shape=(P, 512), dt=F32):
            return ctx.enter_context(nc.psum_tensor(name, list(shape), dt))

        def sem(name):
            return ctx.enter_context(nc.semaphore(name))

        wg = sb("wg", [P, KB, INTER], F16)
        wu = sb("wu", [P, KB, INTER], F16)
        wd = sb("wd", [P, MB, W], F16)
        wqkvl = sb("wqkvl", [P, 4, WIN, C])
        wprev = sb("wprev", [P, WIN, HB])
        wnext = sb("wnext", [P, WIN, HB])
        wproj = sb("wproj", [P, P])
        ident = sb("ident", [P, P])
        pair = sb("pair", [P, P])
        bproj = sb("bproj", [P, C])
        lnw = sb("lnw", [P, C])
        lnb = sb("lnb", [P, C])
        neghalf = sb("neghalf", [P, WIN])
        eps1 = sb("eps1", [P, WIN])
        epsx = sb("epsx", [P, NQ])
        epsc = sb("epsc", [P, 1])
        sgate = sb("sgate", [P, MB])
        sup = sb("sup", [P, MB])
        sdown = sb("sdown", [P, W])
        cbc = sb("cbc", [C, 1])
        pbias = sb("pbias", [P, C])
        msum = sb("msum", [P, 2])
        sprod = sb("sprod", [P, MB])
        top = sb("top", [P, 8])
        ones = sb("ones", [1, P])
        tokens = sb("tokens", [P, WIN + 2])
        xb = sb("xb", [P, WIN, EDGE])
        bst = sb("bst", [P, WIN, 6])
        mv = sb("mv", [P, WIN, 2])
        dmean = sb("dmean", [P, WIN])
        ln1 = sb("ln1", [P, 4, WIN])
        xt = sb("xt", [P, WIN, P])
        qkvl = sb("qkvl", [P, SLICES, WIN, QKVL])
        xl = sb("xl", [P, SLICES, WIN, P])
        prod = sb("prod", [P, 2, 4 * WIN * WIN * HB])
        sum4 = sb("sum4", [P, 2, 1024])
        sum2 = sb("sum2", [P, 2, 512])
        probs = sb("probs", [P, 2, WIN, WIN, WIN])
        smax = sb("smax", [P, 2 * WIN * WIN])
        ssum = sb("ssum", [P, 2 * WIN * WIN])
        attn = sb("attn", [P, 2, WIN, WIN, HB])
        catt = sb("catt", [P, 2, 4, P])
        cent = sb("cent", [P, WIN, WIN, C])
        csq = catt[:].rearrange("p u h (t c) -> p (u h) t c", c=C)
        cvar = sb("cvar", [P, WIN * WIN])
        crs = sb("crs", [P, WIN * WIN])
        ratt = sb("ratt", [P, C, WIN, C])
        early = ratt[:].rearrange("p c h t -> p (c h t)")
        wsm = early[0:C, 0:3 * C]
        wvt = early[0:C, 3 * C:6 * C].rearrange("p (f c) -> p f c", f=3)
        filt = early[0:C, P:P + 2 * HB * 9].rearrange("p (b n) -> p b n", b=2)
        pws = early[0:C, 3 * P:3 * P + C]
        cbr = early[0:C, 4 * P:5 * P]
        spread = early[0:C, 5 * P:6 * P]
        tapped = early[:, 6 * P:7 * P].rearrange("p (s t c) -> p s t c", s=2, t=WIN)
        o1 = sb("o1", [P, NQ, W])
        xr = sb("xr", [P, NQ, W])
        x1 = sb("x1", [P, NQ, W])
        fst = sb("fst", [P, NQ, 6])
        fmv = sb("fmv", [P, 3, NQ, 2])
        frs = sb("frs", [P, 3, 2, NQ])
        yst = sb("yst", [P, NQ, 6])
        xhi = sb("xhi", [P, KB, ROWS], F16)
        xlo = sb("xlo", [P, KB, ROWS], F16)
        gact = sb("gact", [P, 2, ROWS])
        fuse = sb("fuse", [P, 2, ROWS])
        fhi = sb("fhi", [P, 2, ROWS], F16)
        flo = sb("flo", [P, 2, ROWS], F16)
        y = o1

        ps_gate = pb("ps_gate")
        ps_up = pb("ps_up")
        ps_acc = [pb(f"ps_acc{q}") for q in range(NQ)]
        ps_t = pb("ps_t")
        ps_q = pb("ps_q")

        s_const = sem("s_const")
        s_const2 = sem("s_const2")
        s_wload = [sem("s_wload_g"), sem("s_wload_u"), sem("s_wload_d")]
        rows_spread = sem("rows_spread")
        tokens_done = sem("tokens_done")
        blocks_done = sem("blocks_done")
        wvt_done = sem("wvt_done")
        pws_done = sem("pws_done")
        cb_done = sem("cb_done")
        setup_dve = sem("setup_dve")
        bias_done = sem("bias_done")
        top_part = sem("top_part")
        top_row = sem("top_row")
        top_pow2 = sem("top_pow2")
        top_all = sem("top_all")
        scales_set = sem("scales_set")
        lnw_done = sem("lnw_done")
        pool_zero = sem("pool_zero")
        setup_pool = sem("setup_pool")
        w_cast = sem("w_cast")
        t_read = sem("t_read")
        q_read = sem("q_read")
        s_xb = sem("s_xb")
        ln1_chain = sem("ln1_chain")
        ln1_stats = sem("ln1_stats")
        ln1_pair = sem("ln1_pair")
        ln1_var = sem("ln1_var")
        ln1_pool = sem("ln1_pool")
        ln1_rs = sem("ln1_rs")
        xn_done = sem("xn_done")
        xt_tr = sem("xt_tr")
        qkv_done = sem("qkv_done")
        xl_done = sem("xl_done")
        att_chain = sem("att_chain")
        prod_done = sem("prod_done")
        half_done = sem("half_done")
        sub_done = sem("sub_done")
        exp_done = sem("exp_done")
        cat_done = sem("cat_done")
        cat_tr = sem("cat_tr")
        proj_done = sem("proj_done")
        sq_done = sem("sq_done")
        cvar_done = sem("cvar_done")
        crs_chain = sem("crs_chain")
        lnw_chain = sem("lnw_chain")
        crs_done = sem("crs_done")
        cn_done = sem("cn_done")
        ratt_done = sem("ratt_done")
        s_ratt = sem("s_ratt")
        s_o1 = sem("s_o1")
        s_xr = sem("s_xr")
        f_chain = sem("f_chain")
        f_stats = sem("f_stats")
        f_pool = sem("f_pool")
        f_rs = sem("f_rs")
        o1_norm = sem("o1_norm")
        xr_sum = sem("xr_sum")
        fx_done = sem("fx_done")
        fx_tr = sem("fx_tr")
        xhi_done = sem("xhi_done")
        gate_done = sem("gate_done")
        up_done = sem("up_done")
        silu_done = sem("silu_done")
        fuse_done = sem("fuse_done")
        fhi_done = sem("fhi_done")
        flo_done = sem("flo_done")
        down_done = sem("down_done")
        y_chain = sem("y_chain")
        acc_read = sem("acc_read")
        y_stats = sem("y_stats")
        y_pool = sem("y_pool")
        y_rs = sem("y_rs")
        y_norm = sem("y_norm")
        y_sum = sem("y_sum")
        x1_done = sem("x1_done")
        s_out = sem("s_out")

        x_att = x.rearrange("b (s k h a) (e w) -> (b s) e a k h w", s=2, k=NCH, h=WIN, a=4, e=2)
        x_ffn = x.rearrange("b (c s j) n -> b s c j n", c=C, s=2)
        out_ffn = out.rearrange("b (c s j) n -> b s c j n", c=C, s=2)
        r_store = scratch.rearrange("t k c (h a e w) -> t e a k (c h) w", h=WIN, a=4, e=2)
        r_load = scratch.rearrange("t k c (g f) -> t c k g f", g=2)

        def fx_bank(k):
            return ps_t if k % 2 == 0 else ps_q

        def need(eng, s, value):
            if not (isinstance(value, int) and value <= 0):
                eng.wait_ge(s, value)

        SHARE = {"qk": 3.4, "softmax": 3.3, "pv": 3.4, "attn_out": 3.5, "cent_var": 1.2, "cent_out": 1.6,
                 "proj": 0.8, "ln1_stats": 3.5, "ln1_fin": 0.6, "ffn_norm1": 3.2, "ffn_norm2": 3.2}

        def uses_of(step):
            if step[0] in ("xt_transpose", "cat_transpose"):
                return 1, 0
            if step[0] in ("qkv", "proj", "ln1_fin"):
                return 0, 1
            if step[0] == "fx_transpose":
                return (1, 0) if step[2] % 2 == 0 else (0, 1)
            return 0, 0

        def uses(steps):
            return [sum(uses_of(s)[i] for s in steps) for i in (0, 1)]

        def attention_steps(first_half, ahead, cast=()):
            p, a, b = (1, 0), (1, 1), (2, 0)
            cast = [[("cast", 0, i)] for i in cast] + [[]] * 8
            att = []

            def add(*steps):
                att.extend(s for s in steps if ahead or s[1] not in (2, 3, (2, 0), (2, 1)))

            if not first_half:
                return att
            add(("qk", a, 0), ("cat_transpose", p, 0), ("ln1_stats", 2), ("proj", p, 0), ("cat_transpose", p, 1),
                *cast[0], ("qk", a, 1), ("proj", p, 1), ("ln1_fin", 2), *cast[1], ("qk", a, 2), ("cent_var", p),
                ("xt_transpose", (2, 0), 0), *cast[2], ("qk", a, 3), ("xt_transpose", (2, 0), 1), ("softmax", a),
                ("qkv", (2, 0), 0), ("cent_out", p), ("qkv", (2, 0), 1), *cast[3])
            for u in range(UNITS):
                add(("pv", a, u), ("qkv", (2, 0), u + 2), *cast[4 + u])
            add(("attn_out", a), ("qkv", (2, 0), 6), ("qkv", (2, 0), 7), ("token_bias", (2, 0)))
            add(("cat_transpose", a, 0), ("qk", b, 0), ("proj", a, 0), ("cat_transpose", a, 1), ("qk", b, 1),
                ("proj", a, 1), ("xt_transpose", (2, 1), 0), ("qk", b, 2), ("cent_var", a),
                ("xt_transpose", (2, 1), 1), ("qk", b, 3), ("cent_out", a), ("att_store", 1),
                ("qkv", (2, 1), 0), ("softmax", b), ("qkv", (2, 1), 1), ("qkv", (2, 1), 2),
                ("pv", b, 0), ("qkv", (2, 1), 3), ("qkv", (2, 1), 4), ("pv", b, 1), ("qkv", (2, 1), 5),
                ("qkv", (2, 1), 6), ("ffn_norm1", 1), ("qkv", (2, 1), 7), ("token_bias", (2, 1)), ("load_xb", 3),
                ("pv", b, 2), ("pv", b, 3), ("ffn_norm2", 1), ("attn_out", b))
            return att

        def body_steps(first_half=True, ahead=True, before=True):
            att = attention_steps(first_half, ahead)
            share = [SHARE.get(s[0], 0.4) for s in att]
            slots = 3 * MB
            steps, done, slot = [], 0, 0
            for m in range(MB):
                for part in ("gate", "up", "down"):
                    if part != "down":
                        steps.append((part, 0, m))
                    elif m >= 2:
                        steps.append((part, 0, m - 2))
                    if part == "gate" and m >= 1:
                        steps.append(("fuse_split", 0, m - 1))
                    if part == "up" and m == 0:
                        steps += [("finish", -1)] * before
                    if part == "up" and m == 2:
                        steps.append(("keep_x1", 0))
                    slot += 1
                    while done < len(att) and sum(share[:done]) < sum(share) * slot / slots:
                        steps.append(att[done])
                        done += 1
            fx = [("fx_transpose", 1, k) for k in range(KB)] if first_half else [None] * KB
            steps += [fx[0], ("fuse_split", 0, MB - 1), fx[1], ("down", 0, MB - 2), fx[2], fx[3], ("down", 0, MB - 1)]
            return [s for s in steps if s]

        START = [("load_xb", 0), ("ln1_stats", 0), ("blocks", 0), ("ln1_fin", 0)] \
            + [("xt_transpose", (0, 0), u) for u in range(2)] \
            + [("qkv", (0, 0), h) for h in range(8)] + [("token_bias", (0, 0))] \
            + [("qk", (0, 0), 0), ("qk", (0, 0), 1), ("scales", 0)] \
            + [("xt_transpose", (0, 1), u) for u in range(2)] \
            + [("qkv", (0, 1), h) for h in range(8)] + [("token_bias", (0, 1)), ("load_xb", 1)] \
            + [("qk", (0, 0), 2), ("cast", 0, 0), ("cast", 0, 1), ("qk", (0, 0), 3), ("softmax", (0, 0))]
        for u in range(UNITS):
            START += [("pv", (0, 0), u), ("cast", 0, 2 + u)]
        START += [("attn_out", (0, 0))]
        BEFORE = attention_steps(True, True, cast=range(6, 12)) + [("fx_transpose", 1, k) for k in range(KB)]
        FIRST = body_steps(before=False)
        MIDDLE = body_steps()
        LAST2 = body_steps(ahead=False)
        LAST1 = body_steps(first_half=False) + [("finish", 0)]

        def walk(eng, todo):
            used = [0, 0]

            def run(steps, tile):
                for name, where, *rest in steps:
                    u = uses_of((name, where, *rest))
                    if name in todo:
                        at = tile + where if isinstance(where, int) else (tile + where[0], where[1])
                        skip = isinstance(tile, int) and name == "load_xb" and tile + where >= TILES
                        if not skip:
                            todo[name](at, *rest, used[0], used[1])
                    used[0] += u[0]
                    used[1] += u[1]

            run(START, 0)
            run(BEFORE, -1)
            run(FIRST, 0)
            n, before = uses(MIDDLE), list(used)
            with eng.Fori(1, TILES - 3) as t:
                used[:] = [before[i] + n[i] * (t - 1) for i in (0, 1)]
                run(MIDDLE, t)
            used[:] = [before[i] + n[i] * (TILES - 4) for i in (0, 1)]
            run(MIDDLE, TILES - 3)
            run(LAST2, TILES - 2)
            run(LAST1, TILES - 1)

        block = ctx.enter_context(nc.Block())

        @block.sync
        def _(sp):
            def load_xb(t, *_):
                need(sp, xt_tr, 4 * t)
                need(sp, xl_done, 4 * t)
                for e in range(2):
                    for a in range(4):
                        p0 = 64 * e + 16 * a
                        if isinstance(t, int):
                            src = x_att[t, e, a]
                        else:
                            src = x_att[bass.ds(t, 1), e, a].rearrange("o k h w -> (o k) h w")
                        sp.dma_start(xb[p0:p0 + NCH], src).then_inc(s_xb, 16)

            def att_store(t, *_):
                need(sp, ratt_done, 2 * t + 2)
                for e in range(2):
                    for a in range(4):
                        p0 = 64 * e + 16 * a
                        if isinstance(t, int):
                            dst = r_store[t, e, a]
                        else:
                            dst = r_store[bass.ds(t, 1), e, a].rearrange("o k s w -> (o k) s w")
                        sp.dma_start(dst, ratt[p0:p0 + NCH].rearrange("p c h w -> p (c h) w")).then_inc(s_ratt, 16)
                for q in range(NQ):
                    if q == 0:
                        need(sp, x1_done, t)
                    if q == 0 and isinstance(t, int) and t == 0:
                        sp.wait_ge(w_cast, CASTS)
                    if q == 1:
                        need(sp, fx_tr, KB * t)
                    if q == 2:
                        need(sp, s_out, 64 * (t - 1))
                    if isinstance(t, int):
                        src = x_ffn[t // 2, t % 2, 4 * q:4 * q + 4]
                        sp.dma_start(xr[:, q, :], src).then_inc(s_xr, 16)
                    else:
                        src = x_ffn[bass.ds(t // 2, 1), bass.ds(t % 2, 1), 4 * q:4 * q + 4]
                        sp.dma_start(xr[:, q, :], src.rearrange("b s c j n -> (b s c) j n")).then_inc(s_xr, 16)
                sp.wait_ge(s_ratt, 128 * t + 128)
                for c in range(C):
                    src = r_load[t, c] if isinstance(t, int) else r_load[bass.ds(t, 1), c].rearrange("o k g f -> (o k) g f")
                    p0 = c % 4 * (P // 4)
                    sp.dma_start(o1[p0:p0 + P // 4, c // 4, :], src).then_inc(s_o1, 16)

            def finish(t, *_):
                for q in range(NQ):
                    sp.wait_ge(y_sum, NQ * t + q + 1)
                    if isinstance(t, int):
                        dst = out_ffn[t // 2, t % 2, 4 * q:4 * q + 4]
                    else:
                        dst = out_ffn[bass.ds(t // 2, 1), bass.ds(t % 2, 1), 4 * q:4 * q + 4]
                        dst = dst.rearrange("b s c j n -> (b s c) j n")
                    sp.dma_start(dst, y[:, q, :]).then_inc(s_out, 16)

            load_xb(0)
            for staged, w, loaded in zip((x1, xr, o1), (w_gate, w_up, w_down), s_wload):
                rows = w.shape[0] // P
                sp.dma_start(staged[:].rearrange("p q n -> p (q n)").bitcast(I32).rearrange("p (k n) -> p k n", k=rows),
                             w.rearrange("(k p) n -> p k n", p=P)).then_inc(loaded, 16)

            def load_later(t, *_):
                if not (isinstance(t, int) and t == 0):
                    load_xb(t)

            walk(sp, {"load_xb": load_later, "att_store": att_store, "finish": finish})
            sp.wait_ge(s_out, 64 * TILES)
            sp.wait_ge(s_ratt, 128 * TILES)

        @block.tensor
        def _(pe):
            def ln1_fin(t, ut, uq):
                if isinstance(t, int) and t == 0:
                    pe.wait_ge(blocks_done, 1)
                pe.wait_ge(ln1_stats, t + 1)
                need(pe, q_read, uq)
                nc.tensor.matmul(ps_q[:, 0:2 * WIN], pair[:], mv[:].rearrange("p h s -> p (h s)"),
                                 start=True, stop=True).then_inc(ln1_pair, 1)

            def xt_transpose(at, u, ut, uq):
                t, g = at
                pe.wait_ge(xn_done, t + 1)
                need(pe, t_read, ut)
                for i in range(4):
                    mm = nc.tensor.transpose(ps_t[:, P * i:P * i + P], xb[:, 4 * u + i, P * g:P * g + P], ident[:])
                mm.then_inc(xt_tr, 1)

            def qkv(at, h, ut, uq):
                t, g = at
                pe.wait_ge(t_read, ut)
                need(pe, q_read, uq)
                mm = nc.tensor.matmul(ps_q[:], xt[:, h, :], wqkvl[:].rearrange("p g t c -> p (g t c)"),
                                      start=True, stop=False, skip_group_check=True)
                down = ps_q[:, 3 * P:4 * P].rearrange("p (t c) -> p t c", t=WIN)[:, :, HB:C]
                if h >= 1:
                    mm = nc.tensor.matmul(down, xt[:, h - 1, :], wprev[:], start=False, stop=(h == WIN - 1),
                                          skip_group_check=True)
                if h + 1 < WIN:
                    mm = nc.tensor.matmul(down, xt[:, h + 1, :], wnext[:], start=False, stop=True,
                                          skip_group_check=True)
                mm.then_inc(qkv_done, 1)

            def cat_transpose(at, u, ut, uq):
                t, g = at
                pe.wait_ge(cat_done, 2 * t + g + 1)
                need(pe, t_read, ut)
                for i in range(4):
                    mm = nc.tensor.transpose(ps_t[:, P * i:P * i + P], qkvl[:, g, 4 * u + i, 3 * P:4 * P], ident[:])
                mm.then_inc(cat_tr, 1)

            def proj(at, u, ut, uq):
                if isinstance(at[0], int) and at == (0, 0):
                    pe.wait_ge(scales_set, 1)
                pe.wait_ge(t_read, ut)
                need(pe, q_read, uq)
                for i in range(4):
                    mm = nc.tensor.matmul(ps_q[:, P * i:P * i + P], catt[:, u, i, :], wproj[:], start=True, stop=True)
                mm.then_inc(proj_done, 1)

            def fx_transpose(t, k, ut, uq):
                pe.wait_ge(fx_done, NQ * t + NQ)
                need(pe, t_read if k % 2 == 0 else q_read, ut if k % 2 == 0 else uq)
                for q in range(NQ):
                    mm = nc.tensor.transpose(fx_bank(k)[:, P * q:P * q + P], o1[:, q, P * k:P * k + P], ident[:])
                mm.then_inc(fx_tr, 1)

            def gate_or_up(ps, w, done):
                for k in range(KB):
                    for part, xs in enumerate((xhi, xlo)):
                        mm = nc.tensor.matmul(ps[:], w[:, k, :], xs[:, k, :], start=(k == 0 and part == 0),
                                              stop=(k == KB - 1 and part == 1))
                mm.then_inc(done, 1)

            def gate(t, m, ut, uq):
                if m == 0:
                    pe.wait_ge(t_read, ut)
                    pe.wait_ge(q_read, uq)
                need(pe, silu_done, MB * t + m)
                gate_or_up(ps_gate, wg[:, :, P * m:P * m + P], gate_done)

            def up(t, m, ut, uq):
                need(pe, fuse_done, MB * t + m)
                gate_or_up(ps_up, wu[:, :, P * m:P * m + P], up_done)

            def down(t, m, ut, uq):
                pe.wait_ge(flo_done, MB * t + m + 1)
                if m == 0:
                    need(pe, acc_read, NQ * t)
                for part, f in enumerate((fhi, flo)):
                    for q in range(NQ):
                        mm = nc.tensor.matmul(ps_acc[q][:], f[:, m % 2, P * q:P * q + P], wd[:, m, :],
                                              start=(m == 0 and part == 0), stop=(m == MB - 1 and part == 1))
                mm.then_inc(down_done, 1)

            def blocks(t, ut, uq):
                pe.wait_ge(wvt_done, 3)
                nc.tensor.matmul(ps_acc[0][:, 0:3 * C], spread, wsm, start=True, stop=True)
                nc.tensor.matmul(ps_acc[0][:, 3 * C:6 * C], spread, wvt.rearrange("p f c -> p (f c)"),
                                 start=True, stop=True).then_inc(rows_spread, 1)

            def scales(t, ut, uq):
                pe.wait_ge(pws_done, 1)
                nc.tensor.matmul(ps_acc[1][:, 0:C], spread, pws, start=True, stop=True).then_inc(rows_spread, 1)
                pe.wait_ge(cb_done, 1)
                nc.tensor.matmul(ps_up[:, 0:C], cbr, pws, start=True, stop=True).then_inc(bias_done, 1)
                pe.wait_ge(top_part, 1)
                nc.tensor.transpose(ps_gate[0:1, 0:P], top[:, 0:1], ident[:]).then_inc(top_row, 1)
                pe.wait_ge(top_pow2, 1)
                nc.tensor.matmul(ps_acc[2][:, 0:1], ones[:], top[0:1, 2:3], start=True, stop=True).then_inc(top_all, 1)

            pe.wait_ge(setup_pool, SETUP_POOL)
            todo = {"ln1_fin": ln1_fin, "xt_transpose": xt_transpose, "qkv": qkv, "cat_transpose": cat_transpose,
                    "proj": proj, "fx_transpose": fx_transpose, "gate": gate, "up": up, "down": down,
                    "blocks": blocks, "scales": scales}

            def first_gate(t, m, ut, uq):
                if isinstance(t, int) and t == 0 and m == 0:
                    pe.wait_ge(w_cast, CASTS)
                    pe.wait_ge(scales_set, 1)
                gate(t, m, ut, uq)

            todo["gate"] = first_gate
            walk(pe, todo)

        @block.scalar
        def _(act):
            def ln1_fin(t, ut, uq):
                act.wait_ge(ln1_rs, t + 1)
                for h in range(WIN):
                    a = nc.scalar.activation(xb[:, h, :], xb[:, h, :], ACT.Identity, bias=ln1[:, 3, h:h + 1],
                                             scale=ln1[:, 2, h:h + 1])
                a.then_inc(xn_done, 1)

            def xt_transpose(at, u, ut, uq):
                t, g = at
                act.wait_ge(xt_tr, 4 * t + 2 * g + u + 1)
                nc.scalar.activation(xt[:, 4 * u:4 * u + 4, :].rearrange("p h r -> p (h r)"), ps_t[:],
                                     ACT.Copy).then_inc(t_read, 1)

            def qkv(at, h, ut, uq):
                t, g = at
                act.wait_ge(qkv_done, WIN * (2 * t + g) + h + 1)
                if h == 0:
                    need(act, cat_tr, 2 * (2 * t + g) - 2)
                nc.scalar.activation(qkvl[:, g, h, :], ps_q[:], ACT.Copy).then_inc(q_read, 1)

            def softmax(at, ut, uq):
                t, g = at
                act.wait_ge(sub_done, 2 * t + g + 1)
                pr = probs[:].rearrange("p b w i j -> p (b w i j)")
                nc.scalar.activation(pr, pr, ACT.Exp, scale=SOFTMAX_SCALE).then_inc(exp_done, 1)

            def cat_transpose(at, u, ut, uq):
                t, g = at
                act.wait_ge(cat_tr, 2 * (2 * t + g) + u + 1)
                need(act, cvar_done, 2 * t + g)
                nc.scalar.activation(catt[:, u].rearrange("p h r -> p (h r)"), ps_t[:], ACT.Copy).then_inc(t_read, 1)

            def proj(at, u, ut, uq):
                act.wait_ge(q_read, uq + 1)
                part = slice(4 * u, 4 * u + 4)
                nc.scalar.activation(csq[:, part].rearrange("p h t c -> p (h t c)"),
                                     cent[:, part].rearrange("p h t c -> p (h t c)"), ACT.Square).then_inc(sq_done, 1)

            def ffn_norm1(t, ut, uq):
                act.wait_ge(f_rs, 2 * t + 1)
                for q in range(NQ):
                    nc.scalar.activation(o1[:, q, :], o1[:, q, :], ACT.Identity, bias=frs[:, 0, 1, q:q + 1],
                                         scale=frs[:, 0, 0, q:q + 1]).then_inc(o1_norm, 1)

            def ffn_norm2(t, ut, uq):
                act.wait_ge(f_rs, 2 * t + 2)
                for q in range(NQ):
                    nc.scalar.activation(o1[:, q, :], xr[:, q, :], ACT.Identity, bias=frs[:, 1, 1, q:q + 1],
                                         scale=frs[:, 1, 0, q:q + 1]).then_inc(fx_done, 1)

            def fx_transpose(t, k, ut, uq):
                act.wait_ge(fx_tr, KB * t + k + 1)
                nc.scalar.activation(xhi[:, k, :], fx_bank(k)[:], ACT.Copy).then_inc(xhi_done, 1)

            def cent_var(at, ut, uq):
                n = 2 * at[0] + at[1]
                act.wait_ge(cvar_done, n + 1)
                need(act, cn_done, n)
                nc.scalar.activation(crs[:], cvar[:], ACT.Sqrt, bias=epsc[:]).then_inc(crs_done, 1)

            def cast(t, i, ut, uq):
                w, k = i // KB, i % KB
                if k == 0:
                    act.wait_ge(s_wload[w], 16)
                part = slice(k * INTER, k * INTER + INTER)
                staged = (x1, xr, o1)[w][:].rearrange("p q n -> p (q n)").bitcast(I8)
                dst = (wg[:].rearrange("p k n -> p (k n)"), wu[:].rearrange("p k n -> p (k n)"),
                       wd[:].rearrange("p m n -> p (m n)"))[w]
                nc.scalar.activation(dst[:, part], staged[:, part], ACT.Copy).then_inc(w_cast, 1)

            def gate(t, m, ut, uq):
                if isinstance(t, int) and t == 0 and m == 0:
                    act.wait_ge(scales_set, 1)
                act.wait_ge(gate_done, MB * t + m + 1)
                need(act, fuse_done, MB * t + m - 1)
                nc.scalar.activation(gact[:, m % 2, :], ps_gate[:], ACT.Silu,
                                     scale=sgate[:, m:m + 1]).then_inc(silu_done, 1)

            def fuse_split(t, m, ut, uq):
                act.wait_ge(fuse_done, MB * t + m + 1)
                need(act, down_done, MB * t + m - 1)
                nc.scalar.activation(fhi[:, m % 2, :], fuse[:, m % 2, :], ACT.Copy).then_inc(fhi_done, 1)

            def finish(t, ut, uq):
                act.wait_ge(y_rs, t + 1)
                for q in range(NQ):
                    nc.scalar.activation(y[:, q, :], y[:, q, :], ACT.Identity, bias=frs[:, 2, 1, q:q + 1],
                                         scale=frs[:, 2, 0, q:q + 1]).then_inc(y_norm, 1)

            def keep_x1(t, ut, uq):
                need(act, y_sum, NQ * t)
                if isinstance(t, int) and t == 0:
                    act.wait_ge(w_cast, CASTS)
                nc.scalar.activation(x1[:], xr[:], ACT.Copy).then_inc(x1_done, 1)

            act.dma_start(wsm, qkv_w).then_inc(s_const, 16)
            for br, cw in ((0, conv_w0), (1, conv_w1)):
                flat = cw.rearrange("c o y x -> (c o y x)").rearrange("(o n) -> o n", o=1)
                act.dma_start(filt[:, br, :], flat.broadcast_to([C, HB * 9])).then_inc(s_const, 16)
            act.dma_start(pws, proj_w).then_inc(s_const2, 16)
            act.dma_start(cbc[0:HB, :], conv_b0.rearrange("(c o) -> c o", o=1),
                          allow_slow_non_contiguous=True).then_inc(s_const2, 16)
            act.dma_start(cbc[HB:C, :], conv_b1.rearrange("(c o) -> c o", o=1),
                          allow_slow_non_contiguous=True).then_inc(s_const2, 16)
            for dst, src in ((lnb, ln_b), (pbias, proj_b), (lnw, ln_w), (sdown, s_down)):
                n = src.shape[0]
                act.dma_start(dst[:], src.rearrange("(o n) -> o n", o=1).broadcast_to([P, n])).then_inc(s_const2, 16)
            for dst, src in ((sgate, s_gate), (sup, s_up)):
                act.dma_start(dst[:], src.rearrange("(m p) -> p m", p=P),
                              allow_slow_non_contiguous=True).then_inc(s_const2, 16)
            walk(act, {"ln1_fin": ln1_fin, "xt_transpose": xt_transpose, "qkv": qkv, "softmax": softmax,
                       "cat_transpose": cat_transpose, "proj": proj, "ffn_norm1": ffn_norm1,
                       "ffn_norm2": ffn_norm2, "fx_transpose": fx_transpose, "gate": gate,
                       "fuse_split": fuse_split, "finish": finish, "keep_x1": keep_x1, "cent_var": cent_var, "cast": cast})

        @block.gpsimd
        def _(pool):
            def inv_std(rs, nb, var, negmean, eps, chain, base, done):
                n = rs.shape[1]
                nc.gpsimd.tensor_tensor(rs, var, eps[:, 0:n], ALU.add).then_inc(chain, 1)
                pool.wait_ge(chain, base + 1)
                nc.gpsimd.tensor_tensor(rs, rs, neghalf[:, 0:n], ALU.pow).then_inc(chain, 1)
                pool.wait_ge(chain, base + 2)
                nc.gpsimd.tensor_tensor(nb, negmean, rs, ALU.mult).then_inc(done, 1)

            def ln1_fin(t, ut, uq):
                pool.wait_ge(ln1_var, t + 1)
                pool.wait_ge(q_read, uq + 1)
                inv_std(ln1[:, 2, :], ln1[:, 3, :], ln1[:, 0, :], ln1[:, 1, :], eps1, ln1_pool, 2 * t, ln1_rs)

            def token_bias(at, ut, uq):
                t, g = at
                pool.wait_ge(xn_done, t + 1)
                need(pool, ratt_done, 2 * t + g - 1)
                src = xb[:, :, P * g:P * g + P].rearrange("p h (t c) -> p h t c", c=C)
                dst = xl[:, g].rearrange("p h (t c) -> p (h t) c", c=C)
                nc.gpsimd.tensor_tensor(xl[:, g].rearrange("p h (t c) -> p h t c", c=C), src,
                                        lnb[:, None, None, :].broadcast_to([P, WIN, WIN, C]),
                                        ALU.add).then_inc(xl_done, 2)

            def halve(n, u, stage):
                pool.wait_ge(prod_done, 2 * UNITS * n + UNITS * stage + u + 1)
                return prod[:, u % 2, :], sum4[:, u % 2, :]

            def sum4_free(n, u, stage):
                links = [1, 2, 3, 4, 8, 9, 10, 11]
                i = UNITS * stage + u - 2
                need(pool, att_chain, ATT_LINKS * n + links[i] if i >= 0 else ATT_LINKS * (n - 1) + links[i])

            def qk(at, u, ut, uq):
                t, g = at
                n = 2 * t + g
                src, dst = halve(n, u, 0)
                sum4_free(n, u, 0)
                s = src.rearrange("p (s c) -> p s c", c=HB)
                nc.gpsimd.tensor_tensor(dst.rearrange("p (s c) -> p s c", c=4), s[:, :, 0:4], s[:, :, 4:8],
                                        ALU.add).then_inc(half_done, 1)

            def pv(at, u, ut, uq):
                t, g = at
                n = 2 * t + g
                src, dst = halve(n, u, 1)
                sum4_free(n, u, 1)
                s = src.rearrange("p (w jc) -> p w jc", jc=WIN * HB)
                nc.gpsimd.tensor_tensor(dst.rearrange("p (w jc) -> p w jc", jc=4 * HB), s[:, :, 0:4 * HB],
                                        s[:, :, 4 * HB:], ALU.add).then_inc(half_done, 1)

            def cent_out(at, ut, uq):
                t, g = at
                n = 2 * t + g
                pool.wait_ge(cn_done, n + 1)
                nc.gpsimd.tensor_tensor(cent[:].rearrange("p h t c -> p (h t) c"),
                                        cent[:].rearrange("p h t c -> p (h t) c"),
                                        lnw[:, None, :].broadcast_to([P, WIN * WIN, C]), ALU.mult).then_inc(lnw_chain, 1)
                pool.wait_ge(lnw_chain, n + 1)
                pool.wait_ge(xl_done, 2 * n + 2)
                if g == 0:
                    need(pool, s_ratt, 128 * t)
                nc.gpsimd.tensor_tensor(ratt[:, :, :, WIN * g:WIN * g + WIN].rearrange("p c h t -> p h t c"),
                                        cent[:], xl[:, g].rearrange("p h (t c) -> p h t c", c=C),
                                        ALU.add).then_inc(ratt_done, 1)

            def ffn_norm1(t, ut, uq):
                pool.wait_ge(f_stats, 2 * t + 1)
                inv_std(frs[:, 0, 0, :], frs[:, 0, 1, :], fmv[:, 0, :, 1], fmv[:, 0, :, 0], eps1, f_pool, 4 * t, f_rs)
                pool.wait_ge(s_xr, 64 * t + 64)
                for q in range(NQ):
                    pool.wait_ge(o1_norm, NQ * t + q + 1)
                    nc.gpsimd.tensor_tensor(xr[:, q, :], xr[:, q, :], o1[:, q, :], ALU.add).then_inc(xr_sum, 1)

            def ffn_norm2(t, ut, uq):
                pool.wait_ge(f_stats, 2 * t + 2)
                inv_std(frs[:, 1, 0, :], frs[:, 1, 1, :], fmv[:, 1, :, 1], fmv[:, 1, :, 0], epsx, f_pool, 4 * t + 2,
                        f_rs)

            def finish(t, ut, uq):
                pool.wait_ge(y_stats, t + 1)
                inv_std(frs[:, 2, 0, :], frs[:, 2, 1, :], fmv[:, 2, :, 1], fmv[:, 2, :, 0], eps1, y_pool, 2 * t, y_rs)
                pool.wait_ge(x1_done, t + 1)
                for q in range(NQ):
                    pool.wait_ge(y_norm, NQ * t + q + 1)
                    nc.gpsimd.tensor_tensor(y[:, q, :], y[:, q, :], x1[:, q, :], ALU.add).then_inc(y_sum, 1)

            for const, value in ((ident, 0.0), (pair, 0.0), (spread, 0.0), (tokens, 1.0), (neghalf, -0.5), (eps1, EPS),
                                 (epsx, EPS * XSCALE ** -2), (epsc, EPS * C)):
                nc.gpsimd.memset(const[:], value).then_inc(pool_zero, 1)
            pool.wait_ge(pool_zero, 8)
            nc.gpsimd.affine_select(out=ident[:], in_=ident[:], compare_op=ALU.not_equal, fill=1.0, base=0,
                                    pattern=[[-1, P]], channel_multiplier=1).then_inc(setup_pool, 1)
            spread3 = spread.rearrange("p (t c) -> p t c", c=C)
            nc.gpsimd.affine_select(out=spread3, in_=spread3, compare_op=ALU.not_equal, fill=1.0, base=0,
                                    pattern=[[0, WIN], [-1, C]], channel_multiplier=1).then_inc(setup_pool, 1)
            nc.gpsimd.affine_select(out=tokens[:], in_=tokens[:], compare_op=ALU.is_ge, fill=0.0, base=C,
                                    pattern=[[-C, WIN + 2]], channel_multiplier=1).then_inc(pool_zero, 1)
            pool.wait_ge(pool_zero, 9)
            nc.gpsimd.affine_select(out=tokens[:], in_=tokens[:], compare_op=ALU.is_ge, fill=0.0, base=-1,
                                    pattern=[[C, WIN + 2]], channel_multiplier=-1).then_inc(tokens_done, 1)
            for i, off in enumerate((0, 64, -64)):
                if i:
                    pool.wait_ge(setup_pool, 2 + i)
                nc.gpsimd.affine_select(out=pair[:], in_=pair[:], compare_op=ALU.not_equal, fill=0.5, base=off,
                                        pattern=[[-1, P]], channel_multiplier=1).then_inc(setup_pool, 1)

            def token_bias_first(at, ut, uq):
                if isinstance(at[0], int) and at == (0, 0):
                    pool.wait_ge(s_const2, 16 * LATER)
                token_bias(at, ut, uq)

            def cent_out_first(at, ut, uq):
                if isinstance(at[0], int) and at == (0, 0):
                    pool.wait_ge(lnw_done, 1)
                cent_out(at, ut, uq)

            walk(pool, {"ln1_fin": ln1_fin, "token_bias": token_bias_first, "qk": qk, "pv": pv,
                        "cent_out": cent_out_first, "ffn_norm1": ffn_norm1, "ffn_norm2": ffn_norm2, "finish": finish})

        @block.vector
        def _(dve):
            def mean_var(st, n, mean, var, chain, base, done, sign, scale=1.0):
                dve.wait_ge(chain, base + 1)
                nc.vector.tensor_tensor(mean, st[:, :, 1], st[:, :, 4], ALU.add)
                nc.vector.tensor_tensor(st[:, :, 0], st[:, :, 1], st[:, :, 4], ALU.subtract)
                nc.vector.tensor_tensor(st[:, :, 3], st[:, :, 2], st[:, :, 5], ALU.add).then_inc(chain, 1)
                dve.wait_ge(chain, base + 2)
                nc.vector.tensor_scalar(mean, mean, 0.5 * sign, None, ALU.mult)
                nc.vector.scalar_tensor_tensor(st[:, :, 0], st[:, :, 0], 0.25 * scale, st[:, :, 0], ALU.mult,
                                               ALU.mult).then_inc(chain, 1)
                dve.wait_ge(chain, base + 3)
                nc.vector.scalar_tensor_tensor(var, st[:, :, 3], scale / n, st[:, :, 0], ALU.mult,
                                               ALU.add).then_inc(done, 1)

            def ln1_stats_(t, ut, uq):
                dve.wait_ge(s_xb, 128 * t + 128)
                for h in range(WIN):
                    a = nc.vector.bn_stats(bst[:, h, :], xb[:, h, :])
                a.then_inc(ln1_chain, 1)
                mean_var(bst, EDGE, mv[:, :, 0], mv[:, :, 1], ln1_chain, 5 * t, ln1_stats, 1.0)

            def ln1_fin(t, ut, uq):
                dve.wait_ge(ln1_pair, t + 1)
                avg = ps_q[:, 0:2 * WIN].rearrange("p (h s) -> p h s", s=2)
                nc.vector.tensor_tensor(dmean[:], mv[:, :, 0], avg[:, :, 0], ALU.subtract).then_inc(ln1_chain, 1)
                dve.wait_ge(ln1_chain, 5 * t + 4)
                nc.vector.tensor_tensor(dmean[:], dmean[:], dmean[:], ALU.mult).then_inc(ln1_chain, 1)
                dve.wait_ge(ln1_chain, 5 * t + 5)
                nc.vector.tensor_tensor(ln1[:, 0, :], dmean[:], avg[:, :, 1], ALU.add).then_inc(ln1_var, 1)
                nc.vector.tensor_scalar(ln1[:, 1, :], avg[:, :, 0], -1.0, None, ALU.mult).then_inc(q_read, 1)

            def window(g, part, br, w):
                v = qkvl[:, g, :, P * part:P * part + P].rearrange("p h (t c) -> p h t c", c=C)
                return v[:, w, :, 0:HB] if br == 0 else v[:, :, w, HB:C]

            def products(at, u, stage, left, right):
                t, g = at
                n = 2 * t + g
                need(dve, half_done, 2 * UNITS * n + UNITS * stage + u - 1)
                for i in range(4):
                    br, w = u // 2, 4 * (u % 2) + i
                    dst = prod[:, u % 2, 512 * i:512 * i + 512].rearrange("p (i j c) -> p i j c", i=WIN, j=WIN)
                    a = nc.vector.tensor_tensor(dst, left(g, br, w), right(g, br, w), ALU.mult)
                a.then_inc(prod_done, 1)

            def reduce_unit(at, u, stage, dst):
                t, g = at
                n = 2 * t + g
                dve.wait_ge(half_done, 2 * UNITS * n + UNITS * stage + u + 1)
                link = ATT_LINKS * n + 7 * stage + u + 1
                if stage == 0:
                    a = sum4[:, u % 2, :].rearrange("p (s c) -> p s c", c=4)
                    b = sum2[:, u % 2, :].rearrange("p (s c) -> p s c", c=2)
                    nc.vector.tensor_tensor(b, a[:, :, 0:2], a[:, :, 2:4], ALU.add).then_inc(att_chain, 1)
                    dve.wait_ge(att_chain, link)
                    return nc.vector.tensor_tensor(dst, b[:, :, 0], b[:, :, 1], ALU.add)
                a = sum4[:, u % 2, :].rearrange("p (w jc) -> p w jc", jc=4 * HB)
                b = sum2[:, u % 2, :].rearrange("p (w jc) -> p w jc", jc=2 * HB)
                nc.vector.tensor_tensor(b, a[:, :, 0:2 * HB], a[:, :, 2 * HB:], ALU.add).then_inc(att_chain, 1)
                dve.wait_ge(att_chain, link)
                return nc.vector.tensor_tensor(dst, b[:, :, 0:HB], b[:, :, HB:], ALU.add)

            def scores_at(u):
                return probs[:, u // 2, 4 * (u % 2):4 * (u % 2) + 4].rearrange("p w i j -> p (w i j)")

            def attn_at(u):
                return attn[:, u // 2, 4 * (u % 2):4 * (u % 2) + 4].rearrange("p w i c -> p (w i) c")

            def qk(at, u, ut, uq):
                t, g = at
                if u == 0:
                    dve.wait_ge(q_read, uq)
                products(at, u, 0,
                         lambda g, br, w: window(g, 0, br, w)[:, :, None, :].broadcast_to([P, WIN, WIN, HB]),
                         lambda g, br, w: window(g, 1, br, w)[:, None, :, :].broadcast_to([P, WIN, WIN, HB]))
                if u >= 1:
                    reduce_unit(at, u - 1, 0, scores_at(u - 1))

            def softmax(at, ut, uq):
                t, g = at
                n = 2 * t + g
                reduce_unit(at, UNITS - 1, 0, scores_at(UNITS - 1)).then_inc(att_chain, 1)
                dve.wait_ge(att_chain, ATT_LINKS * n + 5)
                pr = probs[:].rearrange("p b w i j -> p (b w i) j")
                nc.vector.tensor_reduce(smax[:], pr, AX.X, ALU.max).then_inc(att_chain, 1)
                dve.wait_ge(att_chain, ATT_LINKS * n + 6)
                nc.vector.tensor_tensor(pr, pr, smax[:, :, None].broadcast_to([P, 2 * WIN * WIN, WIN]),
                                        ALU.subtract).then_inc(sub_done, 1)

            def pv(at, u, ut, uq):
                t, g = at
                n = 2 * t + g
                if u == 0:
                    dve.wait_ge(exp_done, n + 1)
                products(at, u, 1,
                         lambda g, br, w: probs[:, br, w][:, :, :, None].broadcast_to([P, WIN, WIN, HB]),
                         lambda g, br, w: window(g, 2, br, w)[:, None, :, :].broadcast_to([P, WIN, WIN, HB]))
                if u == 1:
                    nc.vector.tensor_reduce(ssum[:], probs[:].rearrange("p b w i j -> p (b w i) j"), AX.X,
                                            ALU.add).then_inc(att_chain, 1)
                    dve.wait_ge(att_chain, ATT_LINKS * n + 7)
                    nc.vector.reciprocal(ssum[:], ssum[:])
                if u >= 1:
                    reduce_unit(at, u - 1, 1, attn_at(u - 1))

            def attn_out(at, ut, uq):
                t, g = at
                n = 2 * t + g
                reduce_unit(at, UNITS - 1, 1, attn_at(UNITS - 1)).then_inc(att_chain, 1)
                dve.wait_ge(att_chain, ATT_LINKS * n + 12)
                o = attn[:].rearrange("p b w i c -> p (b w i) c")
                nc.vector.tensor_tensor(o, o, ssum[:, :, None].broadcast_to([P, 2 * WIN * WIN, HB]),
                                        ALU.mult).then_inc(att_chain, 1)
                dve.wait_ge(att_chain, ATT_LINKS * n + 13)
                cat = qkvl[:, g, :, 3 * P:4 * P].rearrange("p h (t c) -> p h t c", c=C)
                nc.vector.tensor_tensor(cat[:, :, :, 0:HB], cat[:, :, :, 0:HB], attn[:, 0], ALU.add)
                cat1 = cat[:, :, :, HB:C].rearrange("p h t c -> p t h c")
                nc.vector.tensor_tensor(cat1, cat1, attn[:, 1], ALU.add).then_inc(cat_done, 1)

            def proj(at, u, ut, uq):
                t, g = at
                dve.wait_ge(proj_done, 2 * (2 * t + g) + u + 1)
                need(dve, ratt_done, 2 * t + g)
                nc.vector.tensor_tensor(cent[:, 4 * u:4 * u + 4].rearrange("p h t c -> p (h t) c"),
                                        ps_q[:].rearrange("p (s c) -> p s c", c=C),
                                        bproj[:, None, :].broadcast_to([P, 4 * WIN, C]), ALU.add).then_inc(q_read, 1)

            def cent_var(at, ut, uq):
                t, g = at
                dve.wait_ge(sq_done, 2 * (2 * t + g) + 2)
                nc.vector.tensor_reduce(cvar[:], csq.rearrange("p h t c -> p (h t) c"), AX.X,
                                        ALU.add).then_inc(cvar_done, 1)

            def cent_out(at, ut, uq):
                t, g = at
                dve.wait_ge(crs_done, 2 * t + g + 1)
                nc.vector.reciprocal(crs[:], crs[:]).then_inc(crs_chain, 1)
                dve.wait_ge(crs_chain, 2 * t + g + 1)
                c = cent[:].rearrange("p h t c -> p (h t) c")
                nc.vector.tensor_tensor(c, c, crs[:, :, None].broadcast_to([P, WIN * WIN, C]),
                                        ALU.mult).then_inc(cn_done, 1)

            def row_stats(src, i, st, chain, base, done, scale=1.0):
                for q in range(NQ):
                    a = nc.vector.bn_stats(st[:, q, :], src[:, q, :])
                a.then_inc(chain, 1)
                mean_var(st, W, fmv[:, i, :, 0], fmv[:, i, :, 1], chain, base, done, -1.0, scale)

            def ffn_norm1(t, ut, uq):
                dve.wait_ge(s_o1, 16 * C * (t + 1))
                row_stats(o1, 0, fst, f_chain, 6 * t, f_stats)

            def ffn_norm2(t, ut, uq):
                dve.wait_ge(xr_sum, NQ * t + NQ)
                row_stats(xr, 1, fst, f_chain, 6 * t + 3, f_stats, XSCALE ** -2)

            def fx_transpose(t, k, ut, uq):
                dve.wait_ge(xhi_done, KB * t + k + 1)
                nc.vector.tensor_tensor(xlo[:, k, :], fx_bank(k)[:], xhi[:, k, :],
                                        ALU.subtract).then_inc(t_read if k % 2 == 0 else q_read, 1)

            def up(t, m, ut, uq):
                dve.wait_ge(up_done, MB * t + m + 1)
                dve.wait_ge(silu_done, MB * t + m + 1)
                need(dve, flo_done, MB * t + m - 1)
                nc.vector.scalar_tensor_tensor(fuse[:, m % 2, :], ps_up[:], sup[:, m:m + 1], gact[:, m % 2, :],
                                               ALU.mult, ALU.mult).then_inc(fuse_done, 1)

            def fuse_split(t, m, ut, uq):
                dve.wait_ge(fhi_done, MB * t + m + 1)
                nc.vector.tensor_tensor(flo[:, m % 2, :], fuse[:, m % 2, :], fhi[:, m % 2, :],
                                        ALU.subtract).then_inc(flo_done, 1)

            def finish(t, ut, uq):
                dve.wait_ge(down_done, MB * t + MB)
                if not (isinstance(t, int) and t == TILES - 1):
                    dve.wait_ge(fx_tr, KB * (t + 2))
                else:
                    dve.wait_ge(s_out, 64 * t)
                for q in range(NQ):
                    nc.vector.tensor_tensor(y[:, q, :], ps_acc[q][:], sdown[:], ALU.mult).then_inc(acc_read, 1)
                dve.wait_ge(acc_read, NQ * t + NQ)
                row_stats(y, 2, yst, y_chain, 3 * t, y_stats)

            nc.vector.memset(ones[:], 1.0).then_inc(wvt_done, 1)
            steps = [0]

            def link(ins):
                steps[0] += 1
                ins.then_inc(setup_dve, 1)
                dve.wait_ge(setup_dve, steps[0])

            dve.wait_ge(s_const, 16 * FIRST_CONSTS)
            for br in range(2):
                f = filt[:, br, :].rearrange("p (c f) -> p f c", f=9)
                part = slice(HB * br, HB * br + HB)
                nc.vector.tensor_tensor(wvt[:, :, part],
                                        wsm[:, None, 2 * C + HB * br:2 * C + HB * br + HB].broadcast_to([C, 3, HB]),
                                        f[:, 3:6, :] if br == 0 else f[:, 1:8:3, :], ALU.mult).then_inc(wvt_done, 1)

            def blocks(t, ut, uq):
                dve.wait_ge(rows_spread, 1)
                dve.wait_ge(tokens_done, 1)
                rows = ps_acc[0][:, 0:6 * C].rearrange("p (f c) -> p f c", c=C)

                def marked(dst, f, chans, s):
                    n = chans.stop - chans.start
                    return nc.vector.tensor_tensor(dst, rows[:, f, None, chans].broadcast_to([P, WIN, n]),
                                                   tokens[:, s:s + WIN, None].broadcast_to([P, WIN, n]), ALU.mult)

                every, low, high = slice(0, C), slice(0, HB), slice(HB, C)
                for part in range(3):
                    marked(wqkvl[:, part], part, every, 1)
                marked(wqkvl[:, 3], 4, every, 1)
                marked(tapped[:, 0], 3, low, 0)
                link(marked(tapped[:, 1], 5, low, 2))
                link(nc.vector.tensor_tensor(wqkvl[:, 3, :, 0:HB], wqkvl[:, 3, :, 0:HB], tapped[:, 0], ALU.add))
                nc.vector.tensor_tensor(wqkvl[:, 3, :, 0:HB], wqkvl[:, 3, :, 0:HB], tapped[:, 1], ALU.add)
                marked(wprev[:], 3, high, 1)
                marked(wnext[:], 5, high, 1).then_inc(blocks_done, 1)

            def scales(t, ut, uq):
                dve.wait_ge(s_const2, 16 * LATER)
                for mat, mean, done in ((pws, msum[0:C, 0:1], pws_done), (pbias[:], msum[:, 1:2], setup_dve)):
                    link(nc.vector.tensor_reduce(mean, mat, AX.X, ALU.add))
                    link(nc.vector.tensor_scalar(mean, mean, 1.0 / C, None, ALU.mult))
                    if mat is pws:
                        nc.vector.tensor_scalar(mat, mat, mean, None, ALU.subtract).then_inc(done, 1)
                    else:
                        link(nc.vector.tensor_scalar(mat, mat, mean, None, ALU.subtract))
                nc.vector.tensor_copy(cbr, cbc[:].broadcast_to([C, P])).then_inc(cb_done, 1)
                nc.vector.tensor_scalar(lnw[:], lnw[:], C ** 0.5, None, ALU.mult).then_inc(lnw_done, 1)
                link(nc.vector.tensor_tensor(sprod[:], sgate[:], sup[:], ALU.mult))
                nc.vector.tensor_reduce(top[:, 0:1], sprod[:], AX.X, ALU.max,
                                        apply_absolute_value=True).then_inc(top_part, 1)
                dve.wait_ge(rows_spread, 2)
                nc.vector.tensor_tensor(wproj[:].rearrange("p (t c) -> p t c", c=C),
                                        ps_acc[1][:, None, 0:C].broadcast_to([P, WIN, C]),
                                        tokens[:, 1:1 + WIN, None].broadcast_to([P, WIN, C]), ALU.mult)
                dve.wait_ge(top_row, 1)
                link(nc.vector.tensor_reduce(top[0:1, 1:2], ps_gate[0:1, 0:P], AX.X, ALU.max))
                link(nc.vector.tensor_scalar(top[0:1, 1:2], top[0:1, 1:2], 2.0 ** -90, None, ALU.max))
                nc.vector.tensor_scalar(top[0:1, 2:3].bitcast(I32), top[0:1, 1:2].bitcast(I32), 0x7F800000, None,
                                        ALU.bitwise_and).then_inc(top_pow2, 1)
                dve.wait_ge(top_all, 1)
                link(nc.vector.tensor_copy(top[:, 3:4], ps_acc[2][:, 0:1]))
                link(nc.vector.reciprocal(top[:, 4:5], top[:, 3:4]))
                nc.vector.tensor_scalar(sup[:], sup[:], top[:, 4:5], 2.0 ** -18 / XSCALE, ALU.mult, ALU.mult)
                nc.vector.tensor_scalar(sdown[:], sdown[:], top[:, 3:4], 2.0 ** 18, ALU.mult, ALU.mult)
                nc.vector.tensor_scalar(sgate[:], sgate[:], 1.0 / XSCALE, None, ALU.mult)
                dve.wait_ge(bias_done, 1)
                nc.vector.tensor_tensor(bproj[:], pbias[:], ps_up[:, 0:C], ALU.add).then_inc(scales_set, 1)
                dve.wait_ge(scales_set, 1)

            walk(dve, {"ln1_stats": ln1_stats_, "ln1_fin": ln1_fin, "qk": qk, "softmax": softmax, "pv": pv,
                       "attn_out": attn_out, "proj": proj, "cent_var": cent_var, "cent_out": cent_out,
                       "ffn_norm1": ffn_norm1, "ffn_norm2": ffn_norm2, "fx_transpose": fx_transpose, "up": up,
                       "fuse_split": fuse_split, "finish": finish, "blocks": blocks, "scales": scales})


_INS = ["L0_attn_x", "L0_attn_qkv_w", "L0_attn_conv_w0", "L0_attn_conv_b0", "L0_attn_conv_w1", "L0_attn_conv_b1",
        "L0_attn_proj_w", "L0_attn_proj_b", "L0_attn_ln_w", "L0_attn_ln_b", "L0_ffn_w_gate", "L0_ffn_w_up",
        "L0_ffn_w_down", "L0_ffn_s_gate", "L0_ffn_s_up", "L0_ffn_s_down"]


def kernel(**inputs):
    import numpy as _np
    import concourse.bacc as _bacc
    from concourse import mybir as _mybir
    from concourse.bass_utils import run_bass_kernel_spmd as _run

    nc = _bacc.Bacc("TRN2", target_bir_lowering=False, num_devices=1)
    arrays, args = {}, []
    for name in _INS:
        a = _np.ascontiguousarray(inputs[name])
        if a.dtype == _np.int8:
            a = a.view(_np.int32)
        arrays[f"in_{name}"] = a
        args.append(nc.dram_tensor(f"in_{name}", a.shape, _mybir.dt.from_np(a.dtype), kind="ExternalInput").ap())
    scratch = nc.dram_tensor("attn_rows", (TILES, NCH, C, 2 * W), F32, kind="Internal").ap()
    out = nc.dram_tensor("out_x", (B, H, W), F32, kind="ExternalOutput").ap()
    sandwich_kernel(nc, *args, scratch, out)
    r = _run(nc, [arrays], core_ids=[0])
    return r.results[0]["out_x"]
```

```python
from contextlib import ExitStack

import concourse.bass as bass
from concourse import mybir

P = 128
B, H, W = 4, 1024, 512
C = 16
HB = C // 2
WIN = 8
INTER = 2048
EPS = 1e-5

ROWS = 512
TILES = B * H // ROWS
NCH = ROWS // (4 * WIN)
EDGE = W // 2
SLICES = 2
NQ = ROWS // P
KB = W // P
MB = INTER // P
QKVL = 4 * P
XSCALE = 2.0 ** 10
SOFTMAX_SCALE = HB ** -0.5

F32 = mybir.dt.float32
F16 = mybir.dt.float16
I8 = mybir.dt.int8
I32 = mybir.dt.int32
ALU = mybir.AluOpType
ACT = mybir.ActivationFunctionType
AX = mybir.AxisListType

UNITS = 4
FIRST_CONSTS = 3
LATER = 9
CASTS = 3 * KB
SETUP_POOL = 4
LAG = 3
SPLITS = 4
ATT_LINKS = 20


def sandwich_kernel(nc, x, qkv_w, conv_w0, conv_b0, conv_w1, conv_b1, proj_w, proj_b, ln_w, ln_b,
                    w_gate, w_up, w_down, s_gate, s_up, s_down, scratch, out):
    with ExitStack() as ctx:
        def sb(name, shape, dt=F32):
            return ctx.enter_context(nc.sbuf_tensor(name, shape, dt))

        def pb(name, shape=(P, 512), dt=F32):
            return ctx.enter_context(nc.psum_tensor(name, list(shape), dt))

        def sem(name):
            return ctx.enter_context(nc.semaphore(name))

        wg = sb("wg", [P, KB, INTER], F16)
        wu = sb("wu", [P, KB, INTER], F16)
        wd = sb("wd", [P, MB, W], F16)
        wqkvl = sb("wqkvl", [P, 4, WIN, C])
        wprev = sb("wprev", [P, WIN, HB])
        wnext = sb("wnext", [P, WIN, HB])
        wproj = sb("wproj", [P, P])
        ident = sb("ident", [P, P])
        pair = sb("pair", [P, P])
        bproj = sb("bproj", [P, C])
        lnw = sb("lnw", [P, C])
        lnb = sb("lnb", [P, C])
        neghalf = sb("neghalf", [P, WIN])
        eps1 = sb("eps1", [P, WIN])
        epsx = sb("epsx", [P, NQ])
        epsc = sb("epsc", [P, 1])
        sgate = sb("sgate", [P, MB])
        sup = sb("sup", [P, MB])
        sdown = sb("sdown", [P, W])
        cbc = sb("cbc", [C, 1])
        pbias = sb("pbias", [P, C])
        msum = sb("msum", [P, 2])
        sprod = sb("sprod", [P, MB])
        top = sb("top", [P, 8])
        ones = sb("ones", [1, P])
        tokens = sb("tokens", [P, WIN + 2])
        xb = sb("xb", [P, WIN, EDGE])
        bst = sb("bst", [P, WIN, 6])
        mv = sb("mv", [P, WIN, 2])
        dmean = sb("dmean", [P, WIN])
        ln1 = sb("ln1", [P, 4, WIN])
        xt = sb("xt", [P, WIN, P])
        qkvl = sb("qkvl", [P, SLICES, WIN, QKVL])
        xl = sb("xl", [P, SLICES, WIN, P])
        prod = sb("prod", [P, 2, 4 * WIN * WIN * HB])
        sum4 = sb("sum4", [P, 2, 1024])
        probs = sb("probs", [P, 2, WIN, WIN, WIN])
        smax = sb("smax", [P, 2, WIN * WIN])
        ssum = sb("ssum", [P, 2 * WIN * WIN])
        attn = sb("attn", [P, 2, WIN, WIN, HB])
        catt = sb("catt", [P, 2, 4, P])
        cent = sb("cent", [P, WIN, WIN, C])
        csq = catt[:].rearrange("p u h (t c) -> p (u h) t c", c=C)
        cvar = sb("cvar", [P, WIN * WIN])
        crs = sb("crs", [P, WIN * WIN])
        ratt = sb("ratt", [P, C, WIN, C])
        early = ratt[:].rearrange("p c h t -> p (c h t)")
        wsm = early[0:C, 0:3 * C]
        wvt = early[0:C, 3 * C:6 * C].rearrange("p (f c) -> p f c", f=3)
        filt = early[0:C, P:P + 2 * HB * 9].rearrange("p (b n) -> p b n", b=2)
        pws = early[0:C, 3 * P:3 * P + C]
        cbr = early[0:C, 4 * P:5 * P]
        spread = early[0:C, 5 * P:6 * P]
        tapped = early[:, 6 * P:7 * P].rearrange("p (s t c) -> p s t c", s=2, t=WIN)
        o1 = sb("o1", [P, NQ, W])
        xr = sb("xr", [P, NQ, W])
        x1 = sb("x1", [P, NQ, W])
        fst = sb("fst", [P, NQ, 6])
        fmv = sb("fmv", [P, 3, NQ, 2])
        frs = sb("frs", [P, 3, 2, NQ])
        yst = sb("yst", [P, NQ, 6])
        xhi = sb("xhi", [P, KB, ROWS], F16)
        xlo = sb("xlo", [P, KB, ROWS], F16)
        gact = sb("gact", [P, 2, ROWS])
        fuse = sb("fuse", [P, 2, ROWS])
        fhi = sb("fhi", [P, SPLITS, ROWS], F16)
        flo = sb("flo", [P, SPLITS, ROWS], F16)
        y = o1

        ps_gate = pb("ps_gate")
        ps_up = pb("ps_up")
        ps_acc = [pb(f"ps_acc{q}") for q in range(NQ)]
        ps_t = pb("ps_t")
        ps_q = pb("ps_q")

        s_const = sem("s_const")
        s_const2 = sem("s_const2")
        s_wload = [sem("s_wload_g"), sem("s_wload_u"), sem("s_wload_d")]
        rows_spread = sem("rows_spread")
        tokens_done = sem("tokens_done")
        blocks_done = sem("blocks_done")
        wvt_done = sem("wvt_done")
        pws_done = sem("pws_done")
        cb_done = sem("cb_done")
        setup_dve = sem("setup_dve")
        bias_done = sem("bias_done")
        top_part = sem("top_part")
        top_row = sem("top_row")
        top_pow2 = sem("top_pow2")
        top_all = sem("top_all")
        scales_set = sem("scales_set")
        lnw_done = sem("lnw_done")
        pool_zero = sem("pool_zero")
        setup_pool = sem("setup_pool")
        w_cast = sem("w_cast")
        t_read = sem("t_read")
        q_read = sem("q_read")
        s_xb = sem("s_xb")
        ln1_chain = sem("ln1_chain")
        ln1_stats = sem("ln1_stats")
        ln1_pair = sem("ln1_pair")
        ln1_var = sem("ln1_var")
        ln1_pool = sem("ln1_pool")
        ln1_rs = sem("ln1_rs")
        xn_done = sem("xn_done")
        xt_tr = sem("xt_tr")
        qkv_done = sem("qkv_done")
        xl_done = sem("xl_done")
        att_chain = sem("att_chain")
        prod_done = sem("prod_done")
        half_done = sem("half_done")
        sub_done = sem("sub_done")
        exp_done = sem("exp_done")
        cat_done = sem("cat_done")
        cat_tr = sem("cat_tr")
        proj_done = sem("proj_done")
        sq_done = sem("sq_done")
        cvar_done = sem("cvar_done")
        crs_chain = sem("crs_chain")
        lnw_chain = sem("lnw_chain")
        crs_done = sem("crs_done")
        cn_done = sem("cn_done")
        ratt_done = sem("ratt_done")
        s_ratt = [sem("s_ratt_lo"), sem("s_ratt_hi")]
        s_o1 = [sem("s_o1_lo"), sem("s_o1_hi")]
        s_xr = sem("s_xr")
        f_chain = sem("f_chain")
        f_stats = sem("f_stats")
        f_pool = sem("f_pool")
        f_rs = sem("f_rs")
        xr_sum = sem("xr_sum")
        fx_done = sem("fx_done")
        fx_tr = sem("fx_tr")
        xhi_done = sem("xhi_done")
        gate_done = sem("gate_done")
        up_done = sem("up_done")
        silu_done = sem("silu_done")
        fuse_done = sem("fuse_done")
        fhi_done = sem("fhi_done")
        flo_done = sem("flo_done")
        down_done = sem("down_done")
        last_down = sem("last_down")
        y_chain = sem("y_chain")
        acc_read = sem("acc_read")
        y_stats = sem("y_stats")
        y_pool = sem("y_pool")
        y_rs = sem("y_rs")
        y_norm = sem("y_norm")
        y_sum = sem("y_sum")
        x1_done = sem("x1_done")
        s_out = sem("s_out")

        x_att = x.rearrange("b (s k h a) (e w) -> (b s) h k (a e) w", s=2, k=NCH, h=WIN, a=4, e=2)
        x_ffn = x.rearrange("b (hi lo s k g) n -> b s hi lo k (g n)", hi=2, lo=HB, s=2, g=2)
        out_ffn = out.rearrange("b (hi lo s k g) n -> b s hi lo k (g n)", hi=2, lo=HB, s=2, g=2)
        r_store = scratch.rearrange("t (c k) (ae n) -> t (k ae) c n", c=C, ae=2 * NQ)
        r_load = scratch.rearrange("t (hi r) (ae g n) -> t hi g r ae n", hi=2, ae=2 * NQ, g=2)

        def bank(i):
            return ps_q if i % 2 == 0 else ps_t

        def bank_read(i):
            return q_read if i % 2 == 0 else t_read

        def need(eng, s, value):
            if not (isinstance(value, int) and value <= 0):
                eng.wait_ge(s, value)

        def uses_of(step):
            if step[0] in ("xt_transpose", "cat_transpose"):
                return 1, 0
            if step[0] == "ln1_fin":
                return 0, 1
            if step[0] in ("qkv", "proj", "fx_transpose"):
                return (0, 1) if step[2] % 2 == 0 else (1, 0)
            return 0, 0

        def uses(steps):
            return [sum(uses_of(s)[i] for s in steps) for i in (0, 1)]

        def attention_steps(ahead):
            p, a, b, c = (1, 0), (1, 1), (2, 0), (2, 1)
            plan = [
                (1, ("qk", a, 0)), (5, ("cat_transpose", p, 0)), (6, ("cat_transpose", p, 1)), (6, ("ln1_stats", 2)),
                (7, ("qk", a, 1)), (8, ("proj", p, 0)), (8, ("proj", p, 1)), (9, ("square", p, 0)),
                (9, ("ln1_fin", 2)), (10, ("square", p, 1)), (10, ("qk_sum", a, 0)), (10, ("qk", a, 2)),
                (10, ("ln1_apply", 2, 0)), (11, ("ln1_apply", 2, 1)), (12, ("cent_var", p)), (12, ("qk_sum", a, 1)),
                (12, ("qk", a, 3)), (13, ("cent_std", p)), (14, ("softmax", a, 0)), (14, ("xt_transpose", b, 0)),
                (15, ("qk_sum", a, 2)), (15, ("qk_sum", a, 3)), (15, ("softmax", a, 1)),
                (15, ("xt_transpose", b, 1)), (16, ("cent_out", p)), (16, ("exp", a, 0)), (16, ("exp", a, 1)),
                (16, ("qkv", b, 0)), (17, ("pv", a, 0)), (17, ("qkv", b, 1)), (17, ("qkv", b, 2)),
                (17, ("qkv", b, 3)), (19, ("pv", a, 1)), (19, ("qkv", b, 4)), (20, ("pv_norm", a)),
                (20, ("pv_sum", a, 0)), (20, ("pv", a, 2)), (20, ("qkv", b, 5)), (21, ("pv_sum", a, 1)),
                (21, ("pv", a, 3)), (21, ("qkv", b, 6)), (22, ("qkv", b, 7)), (23, ("pv_sum", a, 2)),
                (23, ("pv_sum", a, 3)), (23, ("attn_out", a)), (24, ("load_xr", 1)), (25, ("qk", b, 0)),
                (25, ("token_bias", b)), (26, ("cat_transpose", a, 0)), (26, ("qk", b, 1)),
                (27, ("cat_transpose", a, 1)), (27, ("qk_sum", b, 0)), (27, ("qk", b, 2)), (28, ("proj", a, 0)),
                (28, ("proj", a, 1)), (29, ("square", a, 0)), (29, ("square", a, 1)), (29, ("cent_var", a)),
                (29, ("xt_transpose", c, 0)), (30, ("cent_std", a)), (30, ("qk_sum", b, 1)), (30, ("qk", b, 3)),
                (30, ("softmax", b, 0)), (31, ("xt_transpose", c, 1)), (31, ("cent_out", a)), (31, ("att_store", 1)),
                (33, ("qkv", c, 0)), (33, ("qk_sum", b, 2)), (33, ("qk_sum", b, 3)), (33, ("softmax", b, 1)),
                (33, ("exp", b, 0)), (33, ("qkv", c, 1)), (34, ("exp", b, 1)), (34, ("pv", b, 0)),
                (35, ("qkv", c, 2)), (35, ("pv", b, 1)), (37, ("qkv", c, 3)), (37, ("pv_norm", b)),
                (37, ("pv_sum", b, 0)), (37, ("pv", b, 2)), (38, ("qkv", c, 4)), (39, ("qkv", c, 5)),
                (39, ("qkv", c, 6)), (40, ("qkv", c, 7)), (40, ("ffn_norm1", 1)), (41, ("norm1_add", 1)),
                (42, ("token_bias", c)), (42, ("ffn_norm2", 1)), (43, ("load_xb", 3)), (43, ("pv_sum", b, 1)),
                (44, ("pv", b, 3)), (44, ("norm2_apply", 1)), (47, ("fx_transpose", 1, 0)),
                (47, ("fx_transpose", 1, 1)), (48, ("pv_sum", b, 2)), (48, ("fx_transpose", 1, 2)),
                (49, ("pv_sum", b, 3)), (49, ("fx_transpose", 1, 3))]
            if not ahead:
                plan = [
                    (1, ("qk", a, 0)), (3, ("cat_transpose", p, 0)), (4, ("cat_transpose", p, 1)), (4, ("qk", a, 1)),
                    (5, ("proj", p, 0)), (6, ("proj", p, 1)), (7, ("square", p, 0)), (7, ("qk_sum", a, 0)),
                    (7, ("qk", a, 2)), (8, ("square", p, 1)), (9, ("cent_var", p)), (10, ("qk_sum", a, 1)),
                    (10, ("qk", a, 3)), (11, ("cent_std", p)), (13, ("cent_out", p)), (13, ("softmax", a, 0)),
                    (13, ("exp", a, 0)), (14, ("qk_sum", a, 2)), (14, ("qk_sum", a, 3)), (14, ("softmax", a, 1)),
                    (15, ("exp", a, 1)), (15, ("pv", a, 0)), (17, ("pv", a, 1)), (19, ("pv_norm", a)),
                    (20, ("pv_sum", a, 0)), (21, ("pv", a, 2)), (22, ("pv_sum", a, 1)), (22, ("pv", a, 3)),
                    (23, ("pv_sum", a, 2)), (24, ("pv_sum", a, 3)), (24, ("attn_out", a)), (24, ("load_xr", 1)),
                    (28, ("cat_transpose", a, 0)), (29, ("cat_transpose", a, 1)), (29, ("proj", a, 0)),
                    (30, ("proj", a, 1)), (30, ("square", a, 0)), (31, ("square", a, 1)), (31, ("cent_var", a)),
                    (31, ("cent_std", a)), (32, ("cent_out", a)), (33, ("att_store", 1)), (40, ("ffn_norm1", 1)),
                    (43, ("norm1_add", 1)), (46, ("ffn_norm2", 1)), (49, ("norm2_apply", 1)),
                    (49, ("fx_transpose", 1, 0)), (49, ("fx_transpose", 1, 1)), (50, ("fx_transpose", 1, 2)),
                    (50, ("fx_transpose", 1, 3))]
            return plan

        def body_steps(first_half=True, ahead=True, before=True):
            plan = attention_steps(ahead) if first_half else []
            if not before:
                p = (1, 0)
                plan = [(0, ("pv_sum", p, 1)), (0, ("pv", p, 3)), (1, ("pv_sum", p, 2)), (1, ("pv_sum", p, 3)),
                        (1, ("attn_out", p))] \
                    + [(max(slot, 2), step) for slot, step in plan]
            else:
                plan = [(0, ("attn_out", (1, 0)))] * first_half \
                    + [(2, ("finish", -1)), (8, ("finish_apply", -1)), (15, ("finish_add", -1, 0)),
                       (19, ("finish_add", -1, 1))] + plan
            plan.append((21, ("keep_x1", 0)))
            steps = []
            for m in range(MB):
                for i, part in enumerate(("gate", "up", "down")):
                    if part != "down":
                        steps.append((part, 0, m))
                    elif m >= LAG:
                        steps.append((part, 0, m - LAG))
                    if part == "down":
                        steps.append(("fuse", 0, m))
                    steps += [s for slot, s in plan if slot == 3 * m + i]
                    if m >= 1 and part != "down":
                        steps.append(("fuse_hi" if part == "gate" else "fuse_lo", 0, m - 1))
            if not first_half:
                return steps + [("fuse_hi", 0, MB - 1), ("fuse_lo", 0, MB - 1)] \
                    + [("down_last", 0, q) for q in range(NQ)] + [("finish_last", 0, u) for u in range(2)] \
                    + [("finish_apply_last", 0, u) for u in range(2)] + [("finish_add_last", 0, u) for u in range(2)]
            for i in range(LAG):
                steps.append(("down", 0, MB - LAG + i))
                if i == 0:
                    steps += [("fuse_hi", 0, MB - 1), ("fuse_lo", 0, MB - 1)]
                steps += [s for slot, s in plan if slot == 3 * MB + i]
            return steps

        p, a, b, c = (0, 0), (0, 1), (1, 0), (1, 1)
        START = [("load_xb", 0), ("ln1_stats", 0), ("blocks", 0), ("ln1_fin", 0), ("scale_sums", 0), ("scale_row", 0),
                 ("ln1_apply", 0, 0), ("ln1_apply", 0, 1), ("scale_pow2", 0), ("warm", 0, 4), ("xt_transpose", p, 0),
                 ("xt_transpose", p, 1), ("scale_spread", 0), ("scales", 0)] \
            + [("qkv", p, h) for h in range(4)] + [("qk", p, 0)] + [("qkv", p, h) for h in range(4, 8)] \
            + [("token_bias", p), ("qk", p, 1), ("qk_sum", p, 0), ("qk", p, 2), ("qk_sum", p, 1), ("qk", p, 3)] \
            + [("xt_transpose", a, u) for u in range(2)] + [("qkv", a, h) for h in range(2)] \
            + [("softmax", p, 0), ("exp", p, 0), ("qk_sum", p, 2), ("qk_sum", p, 3), ("softmax", p, 1), ("exp", p, 1)] \
            + [("qkv", a, h) for h in range(2, 8)] \
            + [("token_bias", a), ("load_xb", 1), ("pv", p, 0), ("cast", 0, 0), ("pv", p, 1), ("cast", 0, 1),
               ("pv_norm", p), ("pv_sum", p, 0), ("pv", p, 2), ("cast", 0, 2), ("pv_sum", p, 1), ("pv", p, 3),
               ("pv_sum", p, 2), ("pv_sum", p, 3), ("attn_out", p), ("cast", 0, 3)]
        BEFORE = [("qk", a, 0), ("cat_transpose", p, 0), ("cat_transpose", p, 1), ("ln1_stats", 1), ("qk", a, 1),
                  ("proj", p, 0), ("proj", p, 1), ("ln1_fin", 1), ("square", p, 0), ("ln1_apply", 1, 0),
                  ("square", p, 1), ("qk_sum", a, 0), ("qk", a, 2), ("cent_var", p), ("cent_std", p),
                  ("ln1_apply", 1, 1), ("xt_transpose", b, 0), ("qk_sum", a, 1), ("qk", a, 3),
                  ("xt_transpose", b, 1), ("softmax", a, 0), ("exp", a, 0), ("cent_out", p), ("qk_sum", a, 2),
                  ("qk_sum", a, 3), ("softmax", a, 1), ("qkv", b, 0), ("exp", a, 1), ("qkv", b, 1), ("pv", a, 0),
                  ("qkv", b, 2), ("qkv", b, 3), ("cast", 0, 4), ("pv", a, 1), ("qkv", b, 4), ("qkv", b, 5),
                  ("cast", 0, 5), ("pv_norm", a), ("pv_sum", a, 0), ("pv", a, 2), ("qkv", b, 6), ("qkv", b, 7),
                  ("cast", 0, 6), ("pv_sum", a, 1), ("pv", a, 3), ("cast", 0, 7), ("pv_sum", a, 2), ("pv_sum", a, 3),
                  ("attn_out", a), ("load_xr", 0), ("cast", 0, 8), ("qk", b, 0), ("warm_cat", a),
                  ("cat_transpose", a, 0), ("cat_transpose", a, 1), ("token_bias", b), ("proj", a, 0),
                  ("proj", a, 1), ("square", a, 0), ("square", a, 1), ("cent_var", a), ("cent_std", a),
                  ("cent_out", a), ("cast", 0, 9), ("cast", 0, 10), ("cast", 0, 11), ("att_store", 0), ("qk", b, 1),
                  ("qk_sum", b, 0), ("qk", b, 2), ("xt_transpose", c, 0), ("xt_transpose", c, 1), ("qk_sum", b, 1),
                  ("qk", b, 3), ("softmax", b, 0), ("exp", b, 0), ("qk_sum", b, 2), ("qk_sum", b, 3),
                  ("softmax", b, 1), ("qkv", c, 0), ("qkv", c, 1), ("exp", b, 1), ("qkv", c, 2), ("qkv", c, 3),
                  ("qkv", c, 4), ("qkv", c, 5), ("qkv", c, 6), ("qkv", c, 7), ("ffn_norm1", 0), ("pv", b, 0),
                  ("norm1_add", 0), ("ffn_norm2", 0), ("pv", b, 1), ("pv_norm", b), ("pv_sum", b, 0), ("pv", b, 2),
                  ("norm2_apply", 0), ("warm_fx", 0), ("fx_transpose", 0, 0), ("fx_transpose", 0, 1),
                  ("fx_transpose", 0, 2), ("fx_transpose", 0, 3), ("token_bias", c), ("load_xb", 2)]
        FIRST = body_steps(before=False)
        MIDDLE = body_steps()
        LAST2 = body_steps(ahead=False)
        LAST1 = body_steps(first_half=False)

        def walk(eng, todo):
            used = [0, 0]

            def run(steps, tile):
                for name, where, *rest in steps:
                    u = uses_of((name, where, *rest))
                    if name in todo:
                        at = tile + where if isinstance(where, int) else (tile + where[0], where[1])
                        skip = isinstance(tile, int) and name == "load_xb" and tile + where >= TILES
                        if not skip:
                            todo[name](at, *rest, used[0], used[1])
                    used[0] += u[0]
                    used[1] += u[1]

            run(START, 0)
            run(BEFORE, 0)
            run(FIRST, 0)
            n, before = uses(MIDDLE), list(used)
            with eng.Fori(1, TILES - 3) as t:
                used[:] = [before[i] + n[i] * (t - 1) for i in (0, 1)]
                run(MIDDLE, t)
            used[:] = [before[i] + n[i] * (TILES - 4) for i in (0, 1)]
            run(MIDDLE, TILES - 3)
            run(LAST2, TILES - 2)
            run(LAST1, TILES - 1)

        def on_vector(at):
            return isinstance(at[0], int) and at == (0, 1)

        def add_attention(eng, g):
            cat = qkvl[:, g, :, 3 * P:4 * P].rearrange("p h (t c) -> p h t c", c=C)
            eng.tensor_tensor(cat[:, :, :, 0:HB], cat[:, :, :, 0:HB], attn[:, 0], ALU.add)
            cat1 = cat[:, :, :, HB:C].rearrange("p h t c -> p t h c")
            eng.tensor_tensor(cat1, cat1, attn[:, 1], ALU.add).then_inc(cat_done, 1)

        def scale_norm(eng):
            eng.tensor_tensor(cent[:].rearrange("p h t c -> p (h t) c"), cent[:].rearrange("p h t c -> p (h t) c"),
                              lnw[:, None, :].broadcast_to([P, WIN * WIN, C]), ALU.mult).then_inc(lnw_chain, 1)

        def add_token(eng, g):
            token = xl[:, g].rearrange("p h (t c) -> p h t c", c=C)
            for hi in range(2):
                c = slice(HB * hi, HB * hi + HB)
                eng.tensor_tensor(ratt[:, c, :, WIN * g:WIN * g + WIN].rearrange("p c h t -> p h t c"),
                                  cent[:, :, :, c], token[:, :, :, c], ALU.add).then_inc(ratt_done, 1)

        block = ctx.enter_context(nc.Block())

        @block.sync
        def _(sp):
            def load_xb(t, *_):
                need(sp, xt_tr, 4 * t)
                need(sp, xl_done, 4 * t)
                for h in range(WIN):
                    src = x_att[t, h] if isinstance(t, int) else x_att[bass.ds(t, 1), h].rearrange("o k p w -> (o k) p w")
                    sp.dma_start(xb[:, h, :], src).then_inc(s_xb, 16)

            def load_xr(t, *_):
                need(sp, x1_done, t)
                if isinstance(t, int) and t == 0:
                    sp.wait_ge(w_cast, 2 * KB)
                for hi in range(2):
                    if isinstance(t, int):
                        src = x_ffn[t // 2, t % 2, hi]
                    else:
                        src = x_ffn[bass.ds(t // 2, 1), bass.ds(t % 2, 1), hi].rearrange("b s lo k n -> (b s lo) k n")
                    dst = xr[:, 2 * hi:2 * hi + 2, :].rearrange("p q n -> p (q n)")
                    sp.dma_start(dst, src).then_inc(s_xr, 16)

            def att_store(t, *_):
                if isinstance(t, int) and t == 0:
                    sp.wait_ge(w_cast, CASTS)
                need(sp, s_out, 32 * (t - 1))
                dst = r_store[t] if isinstance(t, int) else r_store[bass.ds(t, 1)].rearrange("o p c n -> (o p) c n")
                src = ratt[:].rearrange("p c h w -> p c (h w)")
                for hi in range(2):
                    sp.wait_ge(ratt_done, 4 * t + 3 + hi)
                    part = slice(hi * HB, hi * HB + HB)
                    sp.dma_start(dst[:, part], src[:, part]).then_inc(s_ratt[hi], 16)
                if isinstance(t, int) and t == 1:
                    sp.wait_ge(fx_tr, KB)
                for hi in range(2):
                    sp.wait_ge(s_ratt[hi], 16 * t + 16)
                    for g in range(2):
                        rows = r_load[t, hi, g] if isinstance(t, int) \
                            else r_load[bass.ds(t, 1), hi, g].rearrange("o r ae n -> (o r) ae n")
                        sp.dma_start(o1[:, 2 * hi + g, :].rearrange("p (ae n) -> p ae n", ae=2 * NQ),
                                     rows).then_inc(s_o1[hi], 16)

            def finish_add(t, hi, *_):
                sp.wait_ge(y_sum, NQ * t + 2 * hi + 2)
                if isinstance(t, int):
                    dst = out_ffn[t // 2, t % 2, hi]
                else:
                    dst = out_ffn[bass.ds(t // 2, 1), bass.ds(t % 2, 1), hi].rearrange("b s lo k n -> (b s lo) k n")
                sp.dma_start(dst, y[:, 2 * hi:2 * hi + 2, :].rearrange("p q n -> p (q n)")).then_inc(s_out, 16)

            def finish_add_last(t, u, *_):
                for q in range(2 * u, 2 * u + 2):
                    sp.wait_ge(y_sum, NQ * t + q + 1)
                    dst = out_ffn[t // 2, t % 2, u][:, :, W * (q % 2):W * (q % 2) + W]
                    sp.dma_start(dst, y[:, q, :]).then_inc(s_out, 16)

            load_xb(0)
            sp.wait_ge(s_const2, 16 * LATER)
            for staged, w, loaded in zip((x1, xr, o1), (w_gate, w_up, w_down), s_wload):
                rows = w.shape[0] // P
                sp.dma_start(staged[:].rearrange("p q n -> p (q n)").bitcast(I32).rearrange("p (k n) -> p k n", k=rows),
                             w.rearrange("(k p) n -> p k n", p=P)).then_inc(loaded, 16)

            def load_later(t, *_):
                if not (isinstance(t, int) and t == 0):
                    load_xb(t)

            walk(sp, {"load_xb": load_later, "load_xr": load_xr, "att_store": att_store, "finish_add": finish_add,
                      "finish_add_last": finish_add_last})
            sp.wait_ge(s_out, 32 * (TILES - 1) + 16 * NQ)
            for stored in s_ratt:
                sp.wait_ge(stored, 16 * TILES)

        @block.tensor
        def _(pe):
            def ln1_fin(t, ut, uq):
                if isinstance(t, int) and t == 0:
                    pe.wait_ge(blocks_done, 1)
                pe.wait_ge(ln1_stats, t + 1)
                need(pe, q_read, uq)
                nc.tensor.matmul(ps_q[:, 0:2 * WIN], pair[:], mv[:].rearrange("p h s -> p (h s)"),
                                 start=True, stop=True).then_inc(ln1_pair, 1)

            def xt_transpose(at, u, ut, uq):
                t, g = at
                pe.wait_ge(xn_done, 2 if isinstance(t, int) and t == 0 else 2 * t + u + 1)
                need(pe, t_read, ut)
                for i in range(4):
                    mm = nc.tensor.transpose(ps_t[:, P * i:P * i + P], xb[:, 4 * u + i, P * g:P * g + P], ident[:])
                mm.then_inc(xt_tr, 1)

            def qkv(at, h, ut, uq):
                need(pe, bank_read(h), uq if h % 2 == 0 else ut)
                if h == 0:
                    pe.wait_ge(t_read, ut)
                mm = nc.tensor.matmul(bank(h)[:], xt[:, h, :], wqkvl[:].rearrange("p g t c -> p (g t c)"),
                                      start=True, stop=False, skip_group_check=True)
                down = bank(h)[:, 3 * P:4 * P].rearrange("p (t c) -> p t c", t=WIN)[:, :, HB:C]
                if h >= 1:
                    mm = nc.tensor.matmul(down, xt[:, h - 1, :], wprev[:], start=False, stop=(h == WIN - 1),
                                          skip_group_check=True)
                if h + 1 < WIN:
                    mm = nc.tensor.matmul(down, xt[:, h + 1, :], wnext[:], start=False, stop=True,
                                          skip_group_check=True)
                mm.then_inc(qkv_done, 1)

            def cat_transpose(at, u, ut, uq):
                t, g = at
                pe.wait_ge(cat_done, 2 * t + g + 1)
                need(pe, t_read, ut)
                for i in range(4):
                    mm = nc.tensor.transpose(ps_t[:, P * i:P * i + P], qkvl[:, g, 4 * u + i, 3 * P:4 * P], ident[:])
                mm.then_inc(cat_tr, 1)

            def proj(at, u, ut, uq):
                if isinstance(at[0], int) and at == (0, 0):
                    pe.wait_ge(scales_set, 1)
                pe.wait_ge(t_read, ut)
                if u == 0:
                    need(pe, q_read, uq)
                for i in range(4):
                    mm = nc.tensor.matmul(bank(u)[:, P * i:P * i + P], catt[:, u, i, :], wproj[:], start=True, stop=True)
                mm.then_inc(proj_done, 1)

            def fx_transpose(t, k, ut, uq):
                pe.wait_ge(fx_done, NQ * t + NQ)
                need(pe, bank_read(k), uq if k % 2 == 0 else ut)
                for q in range(NQ):
                    mm = nc.tensor.transpose(bank(k)[:, P * q:P * q + P], o1[:, q, P * k:P * k + P], ident[:])
                mm.then_inc(fx_tr, 1)

            def gate_or_up(ps, w, done):
                for k in range(KB):
                    for part, xs in enumerate((xhi, xlo)):
                        mm = nc.tensor.matmul(ps[:], w[:, k, :], xs[:, k, :], start=(k == 0 and part == 0),
                                              stop=(k == KB - 1 and part == 1))
                mm.then_inc(done, 1)

            def gate(t, m, ut, uq):
                if m == 0:
                    pe.wait_ge(t_read, ut)
                    pe.wait_ge(q_read, uq)
                need(pe, silu_done, MB * t + m)
                gate_or_up(ps_gate, wg[:, :, P * m:P * m + P], gate_done)

            def up(t, m, ut, uq):
                need(pe, fuse_done, MB * t + m)
                gate_or_up(ps_up, wu[:, :, P * m:P * m + P], up_done)

            def down(t, m, ut, uq):
                pe.wait_ge(flo_done, MB * t + m + 1)
                if m == 0:
                    need(pe, acc_read, NQ * t)
                for part, f in enumerate((fhi, flo)):
                    for q in range(NQ):
                        mm = nc.tensor.matmul(ps_acc[q][:], f[:, m % SPLITS, P * q:P * q + P], wd[:, m, :],
                                              start=(m == 0 and part == 0), stop=(m == MB - 1 and part == 1))
                mm.then_inc(down_done, 1)

            def down_last(t, q, ut, uq):
                for m in range(MB - LAG, MB):
                    if q == 0:
                        pe.wait_ge(flo_done, MB * t + m + 1)
                    for part, f in enumerate((fhi, flo)):
                        mm = nc.tensor.matmul(ps_acc[q][:], f[:, m % SPLITS, P * q:P * q + P], wd[:, m, :],
                                              start=False, stop=(m == MB - 1 and part == 1))
                mm.then_inc(last_down, 1)

            def blocks(t, ut, uq):
                pe.wait_ge(wvt_done, 3)
                nc.tensor.matmul(ps_acc[0][:, 0:3 * C], spread, wsm, start=True, stop=True)
                nc.tensor.matmul(ps_acc[0][:, 3 * C:6 * C], spread, wvt.rearrange("p f c -> p (f c)"),
                                 start=True, stop=True).then_inc(rows_spread, 1)

            def scale_row(t, ut, uq):
                pe.wait_ge(pws_done, 1)
                nc.tensor.matmul(ps_acc[1][:, 0:C], spread, pws, start=True, stop=True).then_inc(rows_spread, 1)
                pe.wait_ge(cb_done, 1)
                nc.tensor.matmul(ps_up[:, 0:C], cbr, pws, start=True, stop=True).then_inc(bias_done, 1)
                pe.wait_ge(top_part, 1)
                nc.tensor.transpose(ps_gate[0:1, 0:P], top[:, 0:1], ident[:]).then_inc(top_row, 1)

            def scale_spread(t, ut, uq):
                pe.wait_ge(top_pow2, 1)
                nc.tensor.matmul(ps_acc[2][:, 0:1], ones[:], top[0:1, 2:3], start=True, stop=True).then_inc(top_all, 1)

            pe.wait_ge(setup_pool, SETUP_POOL)

            def warm(t, n, ut, uq):
                for _ in range(n):
                    nc.tensor.matmul(ps_acc[3][:, 0:P], ident[:], ident[:], start=True, stop=True)

            def warm_cat(at, ut, uq):
                pe.wait_ge(att_chain, ATT_LINKS * (2 * at[0] + at[1]) + 18)
                warm(0, 8, ut, uq)

            def warm_fx(t, ut, uq):
                pe.wait_ge(f_stats, 2)
                warm(0, 8, ut, uq)

            todo = {"warm": warm, "warm_cat": warm_cat, "warm_fx": warm_fx,
                    "ln1_fin": ln1_fin, "xt_transpose": xt_transpose, "qkv": qkv, "cat_transpose": cat_transpose,
                    "proj": proj, "fx_transpose": fx_transpose, "gate": gate, "up": up, "down": down,
                    "down_last": down_last, "blocks": blocks, "scale_row": scale_row, "scale_spread": scale_spread}

            def first_gate(t, m, ut, uq):
                if isinstance(t, int) and t == 0 and m == 0:
                    pe.wait_ge(w_cast, CASTS)
                    pe.wait_ge(scales_set, 1)
                gate(t, m, ut, uq)

            todo["gate"] = first_gate
            walk(pe, todo)

        @block.scalar
        def _(act):
            def ln1_apply(t, u, ut, uq):
                if isinstance(t, int) and t == 0 and u == 1:
                    return
                if u == 0:
                    act.wait_ge(ln1_rs, t + 1)
                for h in range(4 * u, 4 * u + 4):
                    a = nc.scalar.activation(xb[:, h, :], xb[:, h, :], ACT.Identity, bias=ln1[:, 3, h:h + 1],
                                             scale=ln1[:, 2, h:h + 1])
                a.then_inc(xn_done, 1)

            def xt_transpose(at, u, ut, uq):
                t, g = at
                act.wait_ge(xt_tr, 4 * t + 2 * g + u + 1)
                nc.scalar.activation(xt[:, 4 * u:4 * u + 4, :].rearrange("p h r -> p (h r)"), ps_t[:],
                                     ACT.Copy).then_inc(t_read, 1)

            def qkv(at, h, ut, uq):
                t, g = at
                act.wait_ge(qkv_done, WIN * (2 * t + g) + h + 1)
                if h == 0:
                    need(act, cat_tr, 2 * (2 * t + g) - 2)
                nc.scalar.activation(qkvl[:, g, h, :], bank(h)[:], ACT.Copy).then_inc(bank_read(h), 1)

            def exp(at, br, ut, uq):
                act.wait_ge(sub_done, 2 * (2 * at[0] + at[1]) + br + 1)
                pr = probs[:, br].rearrange("p w i j -> p (w i j)")
                nc.scalar.activation(pr, pr, ACT.Exp, scale=SOFTMAX_SCALE).then_inc(exp_done, 1)

            def cat_transpose(at, u, ut, uq):
                t, g = at
                act.wait_ge(cat_tr, 2 * (2 * t + g) + u + 1)
                need(act, cvar_done, 2 * t + g)
                nc.scalar.activation(catt[:, u].rearrange("p h r -> p (h r)"), ps_t[:], ACT.Copy).then_inc(t_read, 1)

            def square(at, u, ut, uq):
                act.wait_ge(bank_read(u), uq if u == 0 else ut)
                part = slice(4 * u, 4 * u + 4)
                nc.scalar.activation(csq[:, part].rearrange("p h t c -> p (h t c)"),
                                     cent[:, part].rearrange("p h t c -> p (h t c)"), ACT.Square).then_inc(sq_done, 1)

            def norm2_apply(t, ut, uq):
                act.wait_ge(f_rs, 2 * t + 2)
                for q in range(NQ):
                    nc.scalar.activation(o1[:, q, :], xr[:, q, :], ACT.Identity, bias=frs[:, 1, 1, q:q + 1],
                                         scale=frs[:, 1, 0, q:q + 1]).then_inc(fx_done, 1)

            def fx_transpose(t, k, ut, uq):
                act.wait_ge(fx_tr, KB * t + k + 1)
                nc.scalar.activation(xhi[:, k, :], bank(k)[:], ACT.Copy).then_inc(xhi_done, 1)

            def cent_std(at, ut, uq):
                n = 2 * at[0] + at[1]
                act.wait_ge(cvar_done, n + 1)
                need(act, cn_done, n)
                nc.scalar.activation(crs[:], cvar[:], ACT.Sqrt, bias=epsc[:]).then_inc(crs_done, 1)

            def cast(t, i, ut, uq):
                w, k = i // KB, i % KB
                if k == 0:
                    act.wait_ge(s_wload[w], 16)
                part = slice(k * INTER, k * INTER + INTER)
                staged = (x1, xr, o1)[w][:].rearrange("p q n -> p (q n)").bitcast(I8)
                dst = (wg[:].rearrange("p k n -> p (k n)"), wu[:].rearrange("p k n -> p (k n)"),
                       wd[:].rearrange("p m n -> p (m n)"))[w]
                nc.scalar.activation(dst[:, part], staged[:, part], ACT.Copy).then_inc(w_cast, 1)

            def gate(t, m, ut, uq):
                if isinstance(t, int) and t == 0 and m == 0:
                    act.wait_ge(scales_set, 1)
                act.wait_ge(gate_done, MB * t + m + 1)
                need(act, fuse_done, MB * t + m - 1)
                nc.scalar.activation(gact[:, m % 2, :], ps_gate[:], ACT.Silu,
                                     scale=sgate[:, m:m + 1]).then_inc(silu_done, 1)

            def fuse_hi(t, m, ut, uq):
                act.wait_ge(fuse_done, MB * t + m + 1)
                need(act, down_done, MB * t + m + 1 - SPLITS)
                nc.scalar.activation(fhi[:, m % SPLITS, :], fuse[:, m % 2, :], ACT.Copy).then_inc(fhi_done, 1)

            def finish_apply(t, ut, uq):
                act.wait_ge(y_rs, t + 1)
                for q in range(NQ):
                    nc.scalar.activation(y[:, q, :], y[:, q, :], ACT.Identity, bias=frs[:, 2, 1, q:q + 1],
                                         scale=frs[:, 2, 0, q:q + 1]).then_inc(y_norm, 1)

            def finish_apply_last(t, u, ut, uq):
                act.wait_ge(y_rs, t + u + 1)
                for q in range(2 * u, 2 * u + 2):
                    nc.scalar.activation(y[:, q, :], y[:, q, :], ACT.Identity, bias=frs[:, 2, 1, q:q + 1],
                                         scale=frs[:, 2, 0, q:q + 1]).then_inc(y_norm, 1)

            def keep_x1(t, ut, uq):
                need(act, y_sum, NQ * t)
                if isinstance(t, int) and t == 0:
                    act.wait_ge(w_cast, CASTS)
                for q in range(NQ):
                    a = nc.scalar.activation(x1[:, q, :], xr[:, q, :], ACT.Identity, bias=frs[:, 0, 1, q:q + 1])
                a.then_inc(x1_done, 1)

            act.dma_start(wsm, qkv_w).then_inc(s_const, 16)
            for br, cw in ((0, conv_w0), (1, conv_w1)):
                flat = cw.rearrange("c o y x -> (c o y x)").rearrange("(o n) -> o n", o=1)
                act.dma_start(filt[:, br, :], flat.broadcast_to([C, HB * 9])).then_inc(s_const, 16)
            act.wait_ge(s_const, 16 * FIRST_CONSTS)
            act.dma_start(pws, proj_w).then_inc(s_const2, 16)
            act.dma_start(cbc[0:HB, :], conv_b0.rearrange("(c o) -> c o", o=1),
                          allow_slow_non_contiguous=True).then_inc(s_const2, 16)
            act.dma_start(cbc[HB:C, :], conv_b1.rearrange("(c o) -> c o", o=1),
                          allow_slow_non_contiguous=True).then_inc(s_const2, 16)
            for dst, src in ((lnb, ln_b), (pbias, proj_b), (lnw, ln_w), (sdown, s_down)):
                n = src.shape[0]
                act.dma_start(dst[:], src.rearrange("(o n) -> o n", o=1).broadcast_to([P, n])).then_inc(s_const2, 16)
            for dst, src in ((sgate, s_gate), (sup, s_up)):
                act.dma_start(dst[:], src.rearrange("(m p) -> p m", p=P),
                              allow_slow_non_contiguous=True).then_inc(s_const2, 16)
            walk(act, {"ln1_apply": ln1_apply, "xt_transpose": xt_transpose, "qkv": qkv, "exp": exp,
                       "cat_transpose": cat_transpose, "square": square, "cent_std": cent_std,
                       "norm2_apply": norm2_apply, "fx_transpose": fx_transpose,
                       "gate": gate, "fuse_hi": fuse_hi, "finish_apply": finish_apply,
                       "finish_apply_last": finish_apply_last, "keep_x1": keep_x1,
                       "cast": cast})

        @block.gpsimd
        def _(pool):
            def inv_std(rs, nb, var, negmean, eps, chain, base, done, early=False):
                n = rs.shape[1]
                nc.gpsimd.tensor_tensor(rs, var, eps[:, 0:n], ALU.add).then_inc(chain, 1)
                pool.wait_ge(chain, base + 1)
                nc.gpsimd.tensor_tensor(rs, rs, neghalf[:, 0:n], ALU.pow).then_inc(chain, 1)
                pool.wait_ge(chain, base + 2)
                nc.gpsimd.tensor_tensor(nb, negmean, rs, ALU.mult).then_inc(done, 1)

            def ln1_fin(t, ut, uq):
                pool.wait_ge(ln1_var, t + 1)
                pool.wait_ge(q_read, uq + 1)
                inv_std(ln1[:, 2, :], ln1[:, 3, :], ln1[:, 0, :], ln1[:, 1, :], eps1, ln1_pool, 2 * t, ln1_rs)

            def token_bias(at, ut, uq):
                t, g = at
                pool.wait_ge(xn_done, 2 * t + 2)
                need(pool, ratt_done, 4 * t + 2 * g - 2)
                src = xb[:, :, P * g:P * g + P].rearrange("p h (t c) -> p h t c", c=C)
                dst = xl[:, g].rearrange("p h (t c) -> p (h t) c", c=C)
                nc.gpsimd.tensor_tensor(xl[:, g].rearrange("p h (t c) -> p h t c", c=C), src,
                                        lnb[:, None, None, :].broadcast_to([P, WIN, WIN, C]),
                                        ALU.add).then_inc(xl_done, 2)

            def halve(n, u, stage):
                pool.wait_ge(prod_done, 2 * UNITS * n + UNITS * stage + u + 1)
                return prod[:, u % 2, :], sum4[:, u % 2, :]

            def sum4_free(n, u, stage):
                links = [2, 4, 7, 9, 13, 15, 17, 19]
                i = UNITS * stage + u - 2
                need(pool, att_chain, ATT_LINKS * n + links[i] if i >= 0 else ATT_LINKS * (n - 1) + links[i])

            def qk(at, u, ut, uq):
                t, g = at
                n = 2 * t + g
                src, dst = halve(n, u, 0)
                sum4_free(n, u, 0)
                s = src.rearrange("p (s c) -> p s c", c=HB)
                nc.gpsimd.tensor_tensor(dst.rearrange("p (s c) -> p s c", c=4), s[:, :, 0:4], s[:, :, 4:8],
                                        ALU.add).then_inc(half_done, 1)

            def pv(at, u, ut, uq):
                t, g = at
                n = 2 * t + g
                src, dst = halve(n, u, 1)
                sum4_free(n, u, 1)
                s = src.rearrange("p (w jc) -> p w jc", jc=WIN * HB)
                nc.gpsimd.tensor_tensor(dst.rearrange("p (w jc) -> p w jc", jc=4 * HB), s[:, :, 0:4 * HB],
                                        s[:, :, 4 * HB:], ALU.add).then_inc(half_done, 1)

            def attn_add(at, ut, uq):
                t, g = at
                if on_vector(at):
                    return
                pool.wait_ge(att_chain, ATT_LINKS * (2 * t + g) + 20)
                add_attention(nc.gpsimd, g)

            def cent_out(at, ut, uq):
                t, g = at
                n = 2 * t + g
                if on_vector(at):
                    return
                pool.wait_ge(cn_done, n + 1)
                scale_norm(nc.gpsimd)
                pool.wait_ge(lnw_chain, n + 1)
                pool.wait_ge(xl_done, 2 * n + 2)
                if g == 0:
                    for stored in s_ratt:
                        need(pool, stored, 16 * t)
                add_token(nc.gpsimd, g)

            def ffn_norm1(t, ut, uq):
                pool.wait_ge(f_stats, 2 * t + 1)
                need(pool, x1_done, t)
                inv_std(frs[:, 0, 0, :], frs[:, 0, 1, :], fmv[:, 0, :, 1], fmv[:, 0, :, 0], eps1, f_pool, 4 * t, f_rs)

            def ffn_norm2(t, ut, uq):
                pool.wait_ge(f_stats, 2 * t + 2)
                inv_std(frs[:, 1, 0, :], frs[:, 1, 1, :], fmv[:, 1, :, 1], fmv[:, 1, :, 0], epsx, f_pool, 4 * t + 2,
                        f_rs)

            def finish(t, ut, uq):
                pool.wait_ge(y_stats, t + 1)
                inv_std(frs[:, 2, 0, :], frs[:, 2, 1, :], fmv[:, 2, :, 1], fmv[:, 2, :, 0], eps1, y_pool, 2 * t, y_rs)

            def finish_last(t, u, ut, uq):
                half = slice(2 * u, 2 * u + 2)
                pool.wait_ge(y_stats, t + u + 1)
                inv_std(frs[:, 2, 0, half], frs[:, 2, 1, half], fmv[:, 2, half, 1], fmv[:, 2, half, 0], eps1, y_pool,
                        2 * t + 2 * u, y_rs)

            def finish_add(t, u, ut, uq):
                pool.wait_ge(x1_done, t + 1)
                for q in range(2 * u, 2 * u + 2):
                    pool.wait_ge(y_norm, NQ * t + q + 1)
                    nc.gpsimd.tensor_tensor(y[:, q, :], y[:, q, :], x1[:, q, :], ALU.add).then_inc(y_sum, 1)

            def fuse_lo(t, m, ut, uq):
                pool.wait_ge(fhi_done, MB * t + m + 1)
                need(pool, down_done, MB * t + m + 1 - SPLITS)
                nc.gpsimd.tensor_tensor(flo[:, m % SPLITS, :], fuse[:, m % 2, :], fhi[:, m % SPLITS, :],
                                        ALU.subtract).then_inc(flo_done, 1)

            for const, value in ((ident, 0.0), (pair, 0.0), (spread, 0.0), (tokens, 1.0), (neghalf, -0.5), (eps1, EPS),
                                 (epsx, EPS * XSCALE ** -2), (epsc, EPS * C)):
                nc.gpsimd.memset(const[:], value).then_inc(pool_zero, 1)
            pool.wait_ge(pool_zero, 8)
            nc.gpsimd.affine_select(out=ident[:], in_=ident[:], compare_op=ALU.not_equal, fill=1.0, base=0,
                                    pattern=[[-1, P]], channel_multiplier=1).then_inc(setup_pool, 1)
            spread3 = spread.rearrange("p (t c) -> p t c", c=C)
            nc.gpsimd.affine_select(out=spread3, in_=spread3, compare_op=ALU.not_equal, fill=1.0, base=0,
                                    pattern=[[0, WIN], [-1, C]], channel_multiplier=1).then_inc(setup_pool, 1)
            nc.gpsimd.affine_select(out=tokens[:], in_=tokens[:], compare_op=ALU.is_ge, fill=0.0, base=C,
                                    pattern=[[-C, WIN + 2]], channel_multiplier=1).then_inc(pool_zero, 1)
            pool.wait_ge(pool_zero, 9)
            nc.gpsimd.affine_select(out=tokens[:], in_=tokens[:], compare_op=ALU.is_ge, fill=0.0, base=-1,
                                    pattern=[[C, WIN + 2]], channel_multiplier=-1).then_inc(tokens_done, 1)
            pair3 = pair[:].rearrange("p (r e) -> p r e", e=2)
            for e in range(2):
                if e:
                    pool.wait_ge(setup_pool, 3)
                nc.gpsimd.affine_select(out=pair3, in_=pair3, compare_op=ALU.not_equal, fill=0.5, base=-e,
                                        pattern=[[-2, P // 2], [0, 2]], channel_multiplier=1).then_inc(setup_pool, 1)

            def token_bias_first(at, ut, uq):
                if isinstance(at[0], int) and at == (0, 0):
                    pool.wait_ge(s_const2, 16 * LATER)
                token_bias(at, ut, uq)

            def cent_out_first(at, ut, uq):
                if isinstance(at[0], int) and at == (0, 0):
                    pool.wait_ge(lnw_done, 1)
                cent_out(at, ut, uq)

            walk(pool, {"ln1_fin": ln1_fin, "token_bias": token_bias_first, "qk": qk, "pv": pv, "attn_out": attn_add,
                        "cent_out": cent_out_first, "ffn_norm1": ffn_norm1,
                        "ffn_norm2": ffn_norm2, "finish": finish, "finish_last": finish_last,
                        "finish_add": finish_add, "fuse_lo": fuse_lo})

        @block.vector
        def _(dve):
            def mean_var(st, n, mean, var, chain, base, done, sign, scale=1.0):
                dve.wait_ge(chain, base + 1)
                nc.vector.tensor_tensor(mean, st[:, :, 1], st[:, :, 4], ALU.add)
                nc.vector.tensor_tensor(st[:, :, 0], st[:, :, 1], st[:, :, 4], ALU.subtract)
                nc.vector.tensor_tensor(st[:, :, 3], st[:, :, 2], st[:, :, 5], ALU.add).then_inc(chain, 1)
                dve.wait_ge(chain, base + 2)
                nc.vector.tensor_scalar(mean, mean, 0.5 * sign, None, ALU.mult)
                nc.vector.scalar_tensor_tensor(st[:, :, 0], st[:, :, 0], 0.25 * scale, st[:, :, 0], ALU.mult,
                                               ALU.mult).then_inc(chain, 1)
                dve.wait_ge(chain, base + 3)
                nc.vector.scalar_tensor_tensor(var, st[:, :, 3], scale / n, st[:, :, 0], ALU.mult,
                                               ALU.add).then_inc(done, 1)

            def ln1_stats_(t, ut, uq):
                dve.wait_ge(s_xb, 128 * t + 128)
                for h in range(WIN):
                    a = nc.vector.bn_stats(bst[:, h, :], xb[:, h, :])
                a.then_inc(ln1_chain, 1)
                mean_var(bst, EDGE, mv[:, :, 0], mv[:, :, 1], ln1_chain, 5 * t, ln1_stats, 1.0)

            def ln1_fin(t, ut, uq):
                dve.wait_ge(ln1_pair, t + 1)
                avg = ps_q[:, 0:2 * WIN].rearrange("p (h s) -> p h s", s=2)
                nc.vector.tensor_tensor(dmean[:], mv[:, :, 0], avg[:, :, 0], ALU.subtract).then_inc(ln1_chain, 1)
                dve.wait_ge(ln1_chain, 5 * t + 4)
                nc.vector.tensor_tensor(dmean[:], dmean[:], dmean[:], ALU.mult).then_inc(ln1_chain, 1)
                dve.wait_ge(ln1_chain, 5 * t + 5)
                nc.vector.tensor_tensor(ln1[:, 0, :], dmean[:], avg[:, :, 1], ALU.add).then_inc(ln1_var, 1)
                nc.vector.tensor_scalar(ln1[:, 1, :], avg[:, :, 0], -1.0, None, ALU.mult).then_inc(q_read, 1)

            def ln1_apply(t, u, ut, uq):
                if isinstance(t, int) and t == 0 and u == 1:
                    dve.wait_ge(ln1_rs, 1)
                    for h in range(4, WIN):
                        a = nc.vector.tensor_scalar(xb[:, h, :], xb[:, h, :], ln1[:, 2, h:h + 1], ln1[:, 3, h:h + 1],
                                                    ALU.mult, ALU.add)
                    a.then_inc(xn_done, 1)

            def window(g, part, br, w):
                v = qkvl[:, g, :, P * part:P * part + P].rearrange("p h (t c) -> p h t c", c=C)
                return v[:, w, :, 0:HB] if br == 0 else v[:, :, w, HB:C]

            def products(at, u, stage, left, right, rows_read=None):
                t, g = at
                n = 2 * t + g
                need(dve, half_done, 2 * UNITS * n + UNITS * stage + u - 1)
                for i in range(4):
                    br, w = u // 2, 4 * (u % 2) + i
                    if rows_read:
                        dve.wait_ge(*rows_read[i])
                    dst = prod[:, u % 2, 512 * i:512 * i + 512].rearrange("p (i j c) -> p i j c", i=WIN, j=WIN)
                    a = nc.vector.tensor_tensor(dst, left(g, br, w), right(g, br, w), ALU.mult)
                a.then_inc(prod_done, 1)

            def reduce_unit(at, u, stage, dst):
                t, g = at
                n = 2 * t + g
                dve.wait_ge(half_done, 2 * UNITS * n + UNITS * stage + u + 1)
                link = ATT_LINKS * n + ([1, 3, 6, 8][u] if stage == 0 else 12 + 2 * u)
                if stage == 0:
                    a = sum4[:, u % 2, :].rearrange("p (s c) -> p s c", c=4)
                    lo, hi, one, two = a[:, :, 0:2], a[:, :, 2:4], a[:, :, 0], a[:, :, 1]
                else:
                    a = sum4[:, u % 2, :].rearrange("p (w jc) -> p w jc", jc=4 * HB)
                    lo, hi, one, two = a[:, :, 0:2 * HB], a[:, :, 2 * HB:], a[:, :, 0:HB], a[:, :, HB:2 * HB]
                nc.vector.tensor_tensor(lo, lo, hi, ALU.add).then_inc(att_chain, 1)
                dve.wait_ge(att_chain, link)
                nc.vector.tensor_tensor(dst, one, two, ALU.add).then_inc(att_chain, 1)

            def scores_at(u):
                return probs[:, u // 2, 4 * (u % 2):4 * (u % 2) + 4].rearrange("p w i j -> p (w i j)")

            def attn_at(u):
                return attn[:, u // 2, 4 * (u % 2):4 * (u % 2) + 4].rearrange("p w i c -> p (w i) c")

            def qk(at, u, ut, uq):
                t, g = at
                first = isinstance(t, int) and at == (0, 0)
                if u == 0 and not first:
                    dve.wait_ge(q_read, uq)
                    dve.wait_ge(t_read, ut)
                products(at, u, 0,
                         lambda g, br, w: window(g, 0, br, w)[:, :, None, :].broadcast_to([P, WIN, WIN, HB]),
                         lambda g, br, w: window(g, 1, br, w)[:, None, :, :].broadcast_to([P, WIN, WIN, HB]),
                         rows_read=[(q_read, uq - 1), (t_read, ut - 1), (q_read, uq), (t_read, ut)]
                         if first and u < 2 else None)

            def qk_sum(at, u, ut, uq):
                reduce_unit(at, u, 0, scores_at(u))

            def softmax(at, br, ut, uq):
                t, g = at
                n = 2 * t + g
                dve.wait_ge(att_chain, ATT_LINKS * n + 4 + 5 * br)
                pr = probs[:, br].rearrange("p w i j -> p (w i) j")
                nc.vector.tensor_reduce(smax[:, br, :], pr, AX.X, ALU.max).then_inc(att_chain, 1)
                dve.wait_ge(att_chain, ATT_LINKS * n + 5 + 5 * br)
                nc.vector.tensor_tensor(pr, pr, smax[:, br, :, None].broadcast_to([P, WIN * WIN, WIN]),
                                        ALU.subtract).then_inc(sub_done, 1)

            def pv(at, u, ut, uq):
                t, g = at
                n = 2 * t + g
                if u % 2 == 0:
                    dve.wait_ge(exp_done, 2 * n + u // 2 + 1)
                products(at, u, 1,
                         lambda g, br, w: probs[:, br, w][:, :, :, None].broadcast_to([P, WIN, WIN, HB]),
                         lambda g, br, w: window(g, 2, br, w)[:, None, :, :].broadcast_to([P, WIN, WIN, HB]))

            def pv_norm(at, ut, uq):
                n = 2 * at[0] + at[1]
                dve.wait_ge(exp_done, 2 * n + 2)
                nc.vector.tensor_reduce(ssum[:], probs[:].rearrange("p b w i j -> p (b w i) j"), AX.X,
                                        ALU.add).then_inc(att_chain, 1)
                dve.wait_ge(att_chain, ATT_LINKS * n + 11)
                nc.vector.reciprocal(ssum[:], ssum[:])

            def pv_sum(at, u, ut, uq):
                if u == 0:
                    need(dve, cat_done, 2 * at[0] + at[1])
                reduce_unit(at, u, 1, attn_at(u))

            def attn_out(at, ut, uq):
                t, g = at
                n = 2 * t + g
                dve.wait_ge(att_chain, ATT_LINKS * n + 19)
                o = attn[:].rearrange("p b w i c -> p (b w i) c")
                nc.vector.tensor_tensor(o, o, ssum[:, :, None].broadcast_to([P, 2 * WIN * WIN, HB]),
                                        ALU.mult).then_inc(att_chain, 1)
                if on_vector(at):
                    dve.wait_ge(att_chain, ATT_LINKS * n + 20)
                    add_attention(nc.vector, g)

            def proj(at, u, ut, uq):
                t, g = at
                dve.wait_ge(proj_done, 2 * (2 * t + g) + u + 1)
                need(dve, ratt_done, 4 * t + 2 * g)
                nc.vector.tensor_tensor(cent[:, 4 * u:4 * u + 4].rearrange("p h t c -> p (h t) c"),
                                        bank(u)[:].rearrange("p (s c) -> p s c", c=C),
                                        bproj[:, None, :].broadcast_to([P, 4 * WIN, C]), ALU.add).then_inc(bank_read(u), 1)

            def cent_var(at, ut, uq):
                t, g = at
                dve.wait_ge(sq_done, 2 * (2 * t + g) + 2)
                nc.vector.tensor_reduce(cvar[:], csq.rearrange("p h t c -> p (h t) c"), AX.X,
                                        ALU.add).then_inc(cvar_done, 1)

            def cent_out(at, ut, uq):
                t, g = at
                dve.wait_ge(crs_done, 2 * t + g + 1)
                nc.vector.reciprocal(crs[:], crs[:]).then_inc(crs_chain, 1)
                dve.wait_ge(crs_chain, 2 * t + g + 1)
                c = cent[:].rearrange("p h t c -> p (h t) c")
                nc.vector.tensor_tensor(c, c, crs[:, :, None].broadcast_to([P, WIN * WIN, C]),
                                        ALU.mult).then_inc(cn_done, 1)
                if on_vector(at):
                    n = 2 * t + g
                    dve.wait_ge(cn_done, n + 1)
                    scale_norm(nc.vector)
                    dve.wait_ge(lnw_chain, n + 1)
                    dve.wait_ge(xl_done, 2 * n + 2)
                    add_token(nc.vector, g)

            def row_stats(src, i, st, chain, base, done, scale=1.0, blocks=slice(0, NQ)):
                for q in range(blocks.start, blocks.stop):
                    a = nc.vector.bn_stats(st[:, q, :], src[:, q, :])
                a.then_inc(chain, 1)
                mean_var(st[:, blocks], W, fmv[:, i, blocks, 0], fmv[:, i, blocks, 1], chain, base, done, -1.0, scale)

            def ffn_norm1(t, ut, uq):
                for hi in range(2):
                    dve.wait_ge(s_o1[hi], 32 * (t + 1))
                    for q in (2 * hi, 2 * hi + 1):
                        a = nc.vector.bn_stats(fst[:, q, :], o1[:, q, :])
                a.then_inc(f_chain, 1)
                mean_var(fst, W, fmv[:, 0, :, 0], fmv[:, 0, :, 1], f_chain, 6 * t, f_stats, -1.0)

            def norm1_add(t, ut, uq):
                dve.wait_ge(f_rs, 2 * t + 1)
                dve.wait_ge(s_xr, 32 * t + 32)
                for q in range(NQ):
                    sums = xr[:, q, :].rearrange("p (h ae w) -> p h ae w", h=WIN // 2, w=C)
                    rows = o1[:, q, :].rearrange("p (ae h w) -> p h ae w", h=WIN // 2, w=C)
                    for h in range(WIN // 2):
                        a = nc.vector.scalar_tensor_tensor(sums[:, h], rows[:, h], frs[:, 0, 0, q:q + 1], sums[:, h],
                                                           ALU.mult, ALU.add)
                    a.then_inc(xr_sum, 1)

            def ffn_norm2(t, ut, uq):
                dve.wait_ge(xr_sum, NQ * t + NQ)
                row_stats(xr, 1, fst, f_chain, 6 * t + 3, f_stats, XSCALE ** -2)

            def fx_transpose(t, k, ut, uq):
                dve.wait_ge(xhi_done, KB * t + k + 1)
                nc.vector.tensor_tensor(xlo[:, k, :], bank(k)[:], xhi[:, k, :],
                                        ALU.subtract).then_inc(bank_read(k), 1)

            def fuse_step(t, m, ut, uq):
                dve.wait_ge(up_done, MB * t + m + 1)
                dve.wait_ge(silu_done, MB * t + m + 1)
                need(dve, flo_done, MB * t + m - 1)
                nc.vector.scalar_tensor_tensor(fuse[:, m % 2, :], ps_up[:], sup[:, m:m + 1], gact[:, m % 2, :],
                                               ALU.mult, ALU.mult).then_inc(fuse_done, 1)

            def finish_last(t, u, ut, uq):
                if u == 0:
                    dve.wait_ge(s_out, 32 * t)
                half = slice(2 * u, 2 * u + 2)
                for q in range(half.start, half.stop):
                    dve.wait_ge(last_down, q + 1)
                    nc.vector.tensor_tensor(y[:, q, :], ps_acc[q][:], sdown[:], ALU.mult).then_inc(acc_read, 1)
                dve.wait_ge(acc_read, NQ * t + half.stop)
                row_stats(y, 2, yst, y_chain, 3 * t + 3 * u, y_stats, blocks=half)

            def finish_add_last(t, u, ut, uq):
                dve.wait_ge(x1_done, t + 1)
                for q in range(2 * u, 2 * u + 2):
                    dve.wait_ge(y_norm, NQ * t + q + 1)
                    nc.vector.tensor_tensor(y[:, q, :], y[:, q, :], x1[:, q, :], ALU.add).then_inc(y_sum, 1)

            def finish(t, ut, uq):
                dve.wait_ge(down_done, MB * t + MB)
                dve.wait_ge(fx_tr, KB * (t + 2))
                for q in range(NQ):
                    nc.vector.tensor_tensor(y[:, q, :], ps_acc[q][:], sdown[:], ALU.mult).then_inc(acc_read, 1)
                dve.wait_ge(acc_read, NQ * t + NQ)
                row_stats(y, 2, yst, y_chain, 3 * t, y_stats)

            nc.vector.memset(ones[:], 1.0).then_inc(wvt_done, 1)
            steps = [0]

            def link(ins):
                steps[0] += 1
                ins.then_inc(setup_dve, 1)
                dve.wait_ge(setup_dve, steps[0])

            dve.wait_ge(s_const, 16 * FIRST_CONSTS)
            for br in range(2):
                f = filt[:, br, :].rearrange("p (c f) -> p f c", f=9)
                part = slice(HB * br, HB * br + HB)
                nc.vector.tensor_tensor(wvt[:, :, part],
                                        wsm[:, None, 2 * C + HB * br:2 * C + HB * br + HB].broadcast_to([C, 3, HB]),
                                        f[:, 3:6, :] if br == 0 else f[:, 1:8:3, :], ALU.mult).then_inc(wvt_done, 1)

            def blocks(t, ut, uq):
                dve.wait_ge(rows_spread, 1)
                dve.wait_ge(tokens_done, 1)
                rows = ps_acc[0][:, 0:6 * C].rearrange("p (f c) -> p f c", c=C)

                def marked(dst, f, chans, s):
                    n = chans.stop - chans.start
                    return nc.vector.tensor_tensor(dst, rows[:, f, None, chans].broadcast_to([P, WIN, n]),
                                                   tokens[:, s:s + WIN, None].broadcast_to([P, WIN, n]), ALU.mult)

                every, low, high = slice(0, C), slice(0, HB), slice(HB, C)
                for part in range(3):
                    marked(wqkvl[:, part], part, every, 1)
                marked(wqkvl[:, 3], 4, every, 1)
                marked(tapped[:, 0], 3, low, 0)
                link(marked(tapped[:, 1], 5, low, 2))
                link(nc.vector.tensor_tensor(wqkvl[:, 3, :, 0:HB], wqkvl[:, 3, :, 0:HB], tapped[:, 0], ALU.add))
                nc.vector.tensor_tensor(wqkvl[:, 3, :, 0:HB], wqkvl[:, 3, :, 0:HB], tapped[:, 1], ALU.add)
                marked(wprev[:], 3, high, 1)
                marked(wnext[:], 5, high, 1).then_inc(blocks_done, 1)

            def scale_sums(t, ut, uq):
                dve.wait_ge(s_const2, 16 * LATER)
                for mat, mean, done in ((pws, msum[0:C, 0:1], pws_done), (pbias[:], msum[:, 1:2], setup_dve)):
                    link(nc.vector.tensor_reduce(mean, mat, AX.X, ALU.add))
                    link(nc.vector.tensor_scalar(mean, mean, 1.0 / C, None, ALU.mult))
                    if mat is pws:
                        nc.vector.tensor_scalar(mat, mat, mean, None, ALU.subtract).then_inc(done, 1)
                    else:
                        link(nc.vector.tensor_scalar(mat, mat, mean, None, ALU.subtract))
                nc.vector.tensor_copy(cbr, cbc[:].broadcast_to([C, P])).then_inc(cb_done, 1)
                nc.vector.tensor_scalar(lnw[:], lnw[:], C ** 0.5, None, ALU.mult).then_inc(lnw_done, 1)
                link(nc.vector.tensor_tensor(sprod[:], sgate[:], sup[:], ALU.mult))
                nc.vector.tensor_reduce(top[:, 0:1], sprod[:], AX.X, ALU.max,
                                        apply_absolute_value=True).then_inc(top_part, 1)

            def scale_pow2(t, ut, uq):
                dve.wait_ge(rows_spread, 2)
                nc.vector.tensor_tensor(wproj[:].rearrange("p (t c) -> p t c", c=C),
                                        ps_acc[1][:, None, 0:C].broadcast_to([P, WIN, C]),
                                        tokens[:, 1:1 + WIN, None].broadcast_to([P, WIN, C]), ALU.mult)
                dve.wait_ge(top_row, 1)
                link(nc.vector.tensor_reduce(top[0:1, 1:2], ps_gate[0:1, 0:P], AX.X, ALU.max))
                link(nc.vector.tensor_scalar(top[0:1, 1:2], top[0:1, 1:2], 2.0 ** -90, None, ALU.max))
                nc.vector.tensor_scalar(top[0:1, 2:3].bitcast(I32), top[0:1, 1:2].bitcast(I32), 0x7F800000, None,
                                        ALU.bitwise_and).then_inc(top_pow2, 1)

            def scales(t, ut, uq):
                dve.wait_ge(top_all, 1)
                link(nc.vector.tensor_copy(top[:, 3:4], ps_acc[2][:, 0:1]))
                link(nc.vector.reciprocal(top[:, 4:5], top[:, 3:4]))
                nc.vector.tensor_scalar(sup[:], sup[:], top[:, 4:5], 2.0 ** -18 / XSCALE, ALU.mult, ALU.mult)
                nc.vector.tensor_scalar(sdown[:], sdown[:], top[:, 3:4], 2.0 ** 18, ALU.mult, ALU.mult)
                nc.vector.tensor_scalar(sgate[:], sgate[:], 1.0 / XSCALE, None, ALU.mult)
                dve.wait_ge(bias_done, 1)
                nc.vector.tensor_tensor(bproj[:], pbias[:], ps_up[:, 0:C], ALU.add).then_inc(scales_set, 1)
                dve.wait_ge(scales_set, 1)

            walk(dve, {"ln1_stats": ln1_stats_, "ln1_fin": ln1_fin, "ln1_apply": ln1_apply, "qk": qk, "qk_sum": qk_sum,
                       "softmax": softmax, "pv": pv, "pv_norm": pv_norm,
                       "attn_out": attn_out, "proj": proj, "cent_var": cent_var, "cent_out": cent_out,
                       "ffn_norm1": ffn_norm1, "norm1_add": norm1_add, "ffn_norm2": ffn_norm2,
                       "fx_transpose": fx_transpose, "fuse": fuse_step, "pv_sum": pv_sum,
                       "finish": finish, "blocks": blocks, "scale_sums": scale_sums, "scale_pow2": scale_pow2,
                       "scales": scales, "finish_last": finish_last, "finish_add_last": finish_add_last})


_INS = ["L0_attn_x", "L0_attn_qkv_w", "L0_attn_conv_w0", "L0_attn_conv_b0", "L0_attn_conv_w1", "L0_attn_conv_b1",
        "L0_attn_proj_w", "L0_attn_proj_b", "L0_attn_ln_w", "L0_attn_ln_b", "L0_ffn_w_gate", "L0_ffn_w_up",
        "L0_ffn_w_down", "L0_ffn_s_gate", "L0_ffn_s_up", "L0_ffn_s_down"]


def kernel(**inputs):
    import numpy as _np
    import concourse.bacc as _bacc
    from concourse import mybir as _mybir
    from concourse.bass_utils import run_bass_kernel_spmd as _run

    nc = _bacc.Bacc("TRN2", target_bir_lowering=False, num_devices=1)
    arrays, args = {}, []
    for name in _INS:
        a = _np.ascontiguousarray(inputs[name])
        if a.dtype == _np.int8:
            a = a.view(_np.int32)
        arrays[f"in_{name}"] = a
        args.append(nc.dram_tensor(f"in_{name}", a.shape, _mybir.dt.from_np(a.dtype), kind="ExternalInput").ap())
    scratch = nc.dram_tensor("attn_rows", (TILES, C * NCH, 2 * W), F32, kind="Internal").ap()
    out = nc.dram_tensor("out_x", (B, H, W), F32, kind="ExternalOutput").ap()
    sandwich_kernel(nc, *args, scratch, out)
    r = _run(nc, [arrays], core_ids=[0])
    return r.results[0]["out_x"]
```
